# Optimizing a Trainium2 kernel written in Bass

```python
import numpy as np
import jax
import jax.numpy as jnp

def _softmax(x, axis=-1):
    return jax.nn.softmax(x, axis=axis)

def _gelu(x):
    return jax.nn.gelu(x, approximate=True)

def _silu(x):
    return jax.nn.silu(x)

def _sigmoid(x):
    return jax.nn.sigmoid(x)

def _layernorm(x, axis=-1, eps=1e-05):
    m = jnp.mean(x, axis=axis, keepdims=True)
    v = jnp.var(x, axis=axis, keepdims=True)
    return (x - m) / jnp.sqrt(v + eps)

def _scatter_add(tgt, idx, src, axis=0):
    return tgt.at[idx].add(src)

def _segment_sum(src, seg, n):
    return jax.ops.segment_sum(src, seg, n)
kernel_name = 'mk_xattn_ffn_d1_seqx_r8_8928dd'

def setup_inputs(seed: int=0):
    np.random.seed(seed)
    _w = jnp.asarray

    def _rec_inputs():
        import jax
        import jax.numpy as jnp
        _rk = jax.random.key(seed)
        x = 2.818e-05 + 1 * jax.random.normal(jax.random.fold_in(_rk, 1), (32, 128, 128), jnp.float32)
        _lenS = 128 - jax.random.randint(jax.random.fold_in(_rk, 7), (32,), 0, max(1, 128 // 4) + 1, jnp.int32)
        _lenS2 = 128 - jax.random.randint(jax.random.fold_in(_rk, 8), (32,), 0, max(1, 128 // 4) + 1, jnp.int32)
        _ctx_2048P = jax.random.normal(jax.random.fold_in(_rk, 11), (32, 16, 256), jnp.float32)
        _ctx_2048c = jax.random.dirichlet(jax.random.fold_in(_rk, 511), 0.3 * jnp.ones((16,), jnp.float32), (32, 128))
        _ctx_2048t = jnp.einsum('bsk,bkd->bsd', _ctx_2048c, _ctx_2048P)
        _ctx_2048t = _ctx_2048t * jax.lax.rsqrt(jnp.mean(jnp.square(_ctx_2048t)) + 1e-12) * 0.953939
        ctx_2048 = -0.000125008 + 0.999885 * (_ctx_2048t + 0.3 * jax.random.normal(jax.random.fold_in(_rk, 611), (32, 128, 256), jnp.float32))
        _validS = jnp.arange(128)[None, :] < _lenS[:, None]
        _validS2 = jnp.arange(128)[None, :] < _lenS2[:, None]
        _causal = jnp.tril(jnp.ones((128, 128), dtype=bool))
        mask_BxS2_fk1 = jnp.where(jnp.broadcast_to(_validS2[:, :], (32, 128)), 1.0, 0.0).astype(jnp.float32)
        return (x, ctx_2048, mask_BxS2_fk1)
    x, ctx_2048, mask_BxS2_fk1 = _rec_inputs()

    def _L0_xattn_setup():
        import jax, jax.numpy as jnp
        import numpy as np
        B, S, T = (32, 64, 64)
        SRC_SIZE, TGT_SIZE, OUT_SIZE, NUM_HEAD = (256, 128, 128, 8)
        HEAD_DIM = OUT_SIZE // NUM_HEAD
        key = jax.random.key(seed)
        ks = jax.random.split(key, 12)
        src = jax.random.normal(ks[0], (B, S, SRC_SIZE), dtype=jnp.float32)
        tgt = jax.random.normal(ks[1], (B, T, TGT_SIZE), dtype=jnp.float32)
        src_mask = (jax.random.uniform(ks[2], (B, S)) > 0.3).astype(jnp.float32)
        src_mask = src_mask.at[:, 0].set(1.0)
        tgt_mask = (jax.random.uniform(ks[3], (B, T)) > 0.3).astype(jnp.float32)
        tgt_mask = tgt_mask.at[:, 0].set(1.0)

        def lin(k, out_f, in_f):
            return jax.random.normal(k, (out_f, in_f), dtype=jnp.float32) / np.sqrt(in_f)
        W_src = lin(ks[4], 2 * OUT_SIZE, SRC_SIZE)
        b_src = jnp.zeros((2 * OUT_SIZE,), jnp.float32)
        W_tgt = lin(ks[5], OUT_SIZE, TGT_SIZE)
        b_tgt = jnp.zeros((OUT_SIZE,), jnp.float32)
        W_out = lin(ks[6], OUT_SIZE, OUT_SIZE + TGT_SIZE)
        b_out = jnp.zeros((OUT_SIZE,), jnp.float32)
        return {'src': src, 'tgt': tgt, 'src_mask': src_mask, 'tgt_mask': tgt_mask, 'W_src': W_src, 'b_src': b_src, 'W_tgt': W_tgt, 'b_tgt': b_tgt, 'W_out': W_out, 'b_out': b_out}
    _L0_xattn_all = _L0_xattn_setup()
    _L0_xattn_in = {k: v for k, v in _L0_xattn_all.items() if k in ('W_src', 'b_src', 'W_tgt', 'b_tgt', 'W_out', 'b_out')}
    del _L0_xattn_all

    def _L0_ffn_setup():
        import jax, jax.numpy as jnp
        import numpy as np
        E, TOP_K, D, H = (8, 2, 128, 256)
        B, S = (2, 256)
        key = jax.random.key(seed)
        ks = jax.random.split(key, 10)
        s = 0.02
        return {'x': jax.random.normal(ks[0], (B, S, D), dtype=jnp.float32), 'gate_w': jax.random.normal(ks[1], (E, D), dtype=jnp.float32) * s, 'gate_b': jnp.zeros((E,), dtype=jnp.float32), 'w0': jax.random.normal(ks[2], (E, H, D), dtype=jnp.float32) * s, 'b0': jnp.zeros((E, H), dtype=jnp.float32), 'w1': jax.random.normal(ks[3], (E, H, D), dtype=jnp.float32) * s, 'b1': jnp.zeros((E, H), dtype=jnp.float32), 'w2': jax.random.normal(ks[4], (E, D, H), dtype=jnp.float32) * s, 'b2': jnp.zeros((E, D), dtype=jnp.float32)}
    _L0_ffn_all = _L0_ffn_setup()
    _L0_ffn_in = {k: v for k, v in _L0_ffn_all.items() if k in ('gate_w', 'gate_b', 'w0', 'b0', 'w1', 'b1', 'w2', 'b2')}
    del _L0_ffn_all
    return {'x': x, 'ctx_2048': ctx_2048, 'mask_BxS2_fk1': mask_BxS2_fk1, 'L0_xattn_W_src': _L0_xattn_in['W_src'], 'L0_xattn_b_src': _L0_xattn_in['b_src'], 'L0_xattn_W_tgt': _L0_xattn_in['W_tgt'], 'L0_xattn_b_tgt': _L0_xattn_in['b_tgt'], 'L0_xattn_W_out': _L0_xattn_in['W_out'], 'L0_xattn_b_out': _L0_xattn_in['b_out'], 'L0_ffn_gate_w': _L0_ffn_in['gate_w'], 'L0_ffn_gate_b': _L0_ffn_in['gate_b'], 'L0_ffn_w0': _L0_ffn_in['w0'], 'L0_ffn_b0': _L0_ffn_in['b0'], 'L0_ffn_w1': _L0_ffn_in['w1'], 'L0_ffn_b1': _L0_ffn_in['b1'], 'L0_ffn_w2': _L0_ffn_in['w2'], 'L0_ffn_b2': _L0_ffn_in['b2']}

def reference(x, ctx_2048, mask_BxS2_fk1, L0_xattn_W_src, L0_xattn_b_src, L0_xattn_W_tgt, L0_xattn_b_tgt, L0_xattn_W_out, L0_xattn_b_out, L0_ffn_gate_w, L0_ffn_gate_b, L0_ffn_w0, L0_ffn_b0, L0_ffn_w1, L0_ffn_b1, L0_ffn_w2, L0_ffn_b2):
    import jax
    import jax.numpy as jnp

    def _L0_xattn_ref(src, tgt, src_mask, tgt_mask, W_src, b_src, W_tgt, b_tgt, W_out, b_out):
        import jax, jax.numpy as jnp
        import numpy as np
        B, S, T = (32, 64, 64)
        SRC_SIZE, TGT_SIZE, OUT_SIZE, NUM_HEAD = (256, 128, 128, 8)
        HEAD_DIM = OUT_SIZE // NUM_HEAD
        b, s, _ = src.shape
        t = tgt.shape[1]
        src_trans = jnp.einsum('bsf,of->bso', src, W_src) + b_src
        tgt_trans = jnp.einsum('btf,of->bto', tgt, W_tgt) + b_tgt
        src_trans = src_trans * src_mask[:, :, None]
        tgt_trans = tgt_trans * tgt_mask[:, :, None]
        src_key, src_val = jnp.split(src_trans, 2, axis=2)
        k = src_key.reshape(b, s, NUM_HEAD, HEAD_DIM)
        v = src_val.reshape(b, s, NUM_HEAD, HEAD_DIM)
        q = tgt_trans.reshape(b, t, NUM_HEAD, HEAD_DIM)
        scores = jnp.einsum('bthd,bshd->bhts', q, k) / np.sqrt(HEAD_DIM)
        scores = jnp.where(src_mask[:, None, None, :] == 0, -jnp.inf, scores)
        attn = jax.nn.softmax(scores, axis=-1)
        tgt_update = jnp.einsum('bhts,bshd->bthd', attn, v).reshape(b, t, OUT_SIZE)
        cat_tgt = jnp.concatenate([tgt, tgt_update], axis=2)
        return jnp.einsum('btf,of->bto', cat_tgt, W_out) + b_out

    def _L0_ffn_ref(x, gate_w, gate_b, w0, b0, w1, b1, w2, b2):
        import jax, jax.numpy as jnp
        import numpy as np
        E, TOP_K, D, H = (8, 2, 128, 256)
        B, S = (2, 256)
        Bn, Sq, Dv = x.shape
        xt = x.reshape(-1, Dv)
        logits = xt @ gate_w.T + gate_b
        top_v, top_i = jax.lax.top_k(logits, TOP_K)
        h0 = jnp.einsum('td,ehd->eth', xt, w0) + b0[:, None, :]
        h1 = jnp.einsum('td,ehd->eth', xt, w1) + b1[:, None, :]
        act = h0 * jax.nn.silu(h1)
        out_all = jnp.einsum('eth,edh->etd', act, w2) + b2[:, None, :]
        out_te = jnp.transpose(out_all, (1, 0, 2))
        sel = jnp.take_along_axis(out_te, top_i[:, :, None], axis=1)
        w = jax.nn.softmax(top_v, axis=-1)[:, :, None]
        out = (w * sel).sum(axis=1)
        return out.reshape(Bn, Sq, Dv)
    x = x + _L0_xattn_ref(ctx_2048, _layernorm(x, axis=-1), mask_BxS2_fk1, mask_BxS2_fk1, L0_xattn_W_src, L0_xattn_b_src, L0_xattn_W_tgt, L0_xattn_b_tgt, L0_xattn_W_out, L0_xattn_b_out)
    x = x + _L0_ffn_ref(_layernorm(x, axis=-1), L0_ffn_gate_w, L0_ffn_gate_b, L0_ffn_w0, L0_ffn_b0, L0_ffn_w1, L0_ffn_b1, L0_ffn_w2, L0_ffn_b2)
    return x

_drawn_inputs = setup_inputs


def setup_inputs(seed=0):
    import zlib

    import numpy as np

    out = dict(_drawn_inputs(seed))
    spreads = {'L0_xattn_b_src': (0.0, 0.1),
     'L0_xattn_b_tgt': (0.0, 0.608),
     'L0_xattn_b_out': (0.0, 0.1),
     'L0_ffn_gate_b': (0.0, 0.1),
     'L0_ffn_b0': (0.0, 0.8),
     'L0_ffn_b1': (0.0, 0.8),
     'L0_ffn_b2': (0.0, 0.587)}
    factors = {'L0_ffn_w0': 8.0, 'L0_ffn_w1': 8.0, 'L0_ffn_w2': 8.0}
    for name, (base, spread) in spreads.items():
        noise = np.random.default_rng([zlib.crc32(name.encode()), seed]).standard_normal(out[name].shape)
        drawn = base * np.exp(spread * noise) if base else spread * noise
        out[name] = jnp.asarray(drawn.astype(out[name].dtype))
    for name, factor in factors.items():
        out[name] = (out[name] * factor).astype(out[name].dtype)
    return out
```

```python
from contextlib import ExitStack

import concourse.bass as bass
from concourse import mybir

F32 = mybir.dt.float32
BF16 = mybir.dt.bfloat16
I32 = mybir.dt.int32
ALU = mybir.AluOpType
ACT = mybir.ActivationFunctionType
AX_X = mybir.AxisListType.X

P = 128
B, T, D, DS = 32, 128, 128, 256
HEADS, HD = 8, 16
HALF = HEADS // 2
E, H, TOPK = 8, 256, 2
EPS = 1e-5
FAR = -1.0e30
GROUPS = 2
GB = B // GROUPS
GT = GB * T * TOPK // P + E - 1
TILES = GROUPS * GT
RC = D + 2
NOWHERE = 1 << 20
U = 4

WK, WV, WQ, WO, WG = 0, 2 * D, 4 * D, 5 * D, 7 * D
W_COLS = 7 * D + E
C_IDENT, C_TRI, C_PATT, C_SEL, C_ROW0, C_REV, C_TILE = 0, P, 2 * P, 2 * P + 4, 2 * P + 8, 2 * P + 9, 2 * P + 17
C_COLS = C_TILE + GT
BV, BO, B01, B2 = 0, D, 2 * D, 2 * D + E * 2 * H
BIASES = B2 + E * D


def need(engine, sem, count):
    if not isinstance(count, int) or count > 0:
        engine.wait_ge(sem, count)


def live(b):
    return not isinstance(b, int) or 0 <= b < B


def stand(engine, waits_over):
    engine.sem_inc(waits_over, 1)


def upto(count):
    return min(count, B) if isinstance(count, int) else count


def build(nc, x, ctxT, w_attn, cols, mask_row, gate_b, biases, w01, w2, consts, ids, out):
    with ExitStack() as stack:
        def sb(name, shape, dt=F32):
            return stack.enter_context(nc.sbuf_tensor(name, shape, dt))

        def sem(name):
            return stack.enter_context(nc.semaphore(name))

        xres = sb("xres", [P, B, D])
        rows = sb("rows", [P, B, TOPK, RC])
        ctx = sb("ctx", [P, 4, 2, T])
        wat = sb("wat", [P, W_COLS])
        w01s = sb("w01s", [P, E * 2 * H])
        w2s = sb("w2s", [P, E * 2 * D])
        bias3 = sb("bias3", [P, BIASES], BF16)
        bias_f = sb("bias_f", [P, BIASES // P])
        bias_r = sb("bias_r", [P, 2, BIASES // P])
        bias_p = sb("bias_p", [P, 3, BIASES // P], BF16)
        colsb = sb("colsb", [P, 2 + B])
        maskr = sb("maskr", [P, B * T])
        maskb = sb("maskb", [P, B * T], BF16)
        keyb = sb("keyb", [P, B])
        gbias = sb("gbias", [P, E])
        con = sb("con", [P, C_COLS])
        idsb = sb("idsb", [P, B * TOPK], I32)
        ident_b = sb("ident_b", [P, P], BF16)
        tri_b = sb("tri_b", [P, P], BF16)
        ones_b = sb("ones_b", [P, P], BF16)
        row0_b = sb("row0_b", [P, P], BF16)
        sel_b = sb("sel_b", [P, 4, P], BF16)
        onesf = sb("onesf", [P, P])
        mhalf = sb("mhalf", [P, 1])
        blank = sb("blank", [P, RC])

        st1 = sb("st1", [P, 2, 6])
        mv1 = sb("mv1", [P, 4, 2])
        ve1 = sb("ve1", [P, 4])
        rs1 = sb("rs1", [P, 4])
        st2 = sb("st2", [P, 2, 6])
        mv2 = sb("mv2", [P, 4, 2])
        ve2 = sb("ve2", [P, 4])
        rs2 = sb("rs2", [P, 4])
        xn = sb("xn", [P, 2, D])
        xnT = sb("xnT", [P, 4, T])
        kf = sb("kf", [P, 2, T])
        qf = sb("qf", [P, 2, T])
        kb = sb("kb", [P, 2, T], BF16)
        q4 = sb("q4", [P, 2, HALF, T])
        q4b = sb("q4b", [P, 2, HALF, T], BF16)
        mb = sb("mb", [P, 2, T], BF16)
        nmax = sb("nmax", [P, 2, HEADS])
        mneg = sb("mneg", [P, 2, P], BF16)
        mT = sb("mT", [P, 2, T], BF16)
        attn = sb("attn", [P, 2, HEADS, T])
        vaug = sb("vaug", [P, 2, HEADS, HD + 1])
        rsum = sb("rsum", [P, 2, HEADS])
        upd = sb("upd", [P, 2, D])
        updT = sb("updT", [P, 2, T])
        x2n = sb("x2n", [P, 2, D])
        x2T = sb("x2T", [P, 2, T])
        logits = sb("logits", [P, B, E])

        top = sb("top", [P, 2, GB])
        first = sb("first", [P, 2, GB])
        eqs = sb("eqs", [P, GB, E])
        hot = sb("hot", [P, 2, GB, E])
        lower = sb("lower", [P, GB, E])
        gap = sb("gap", [P, GB])
        gexp = sb("gexp", [P, GB])
        gden = sb("gden", [P, GB])
        picked = sb("picked", [P, E, GB])
        running = sb("running", [P, E * GB])
        rowsum = sb("rowsum", [P, E])
        rowsum_b = sb("rowsum_b", [P, E], BF16)
        rowinc = sb("rowinc", [P, E])
        counts = sb("counts", [P, 2 * E])
        place = sb("place", [P, E])
        cnt_i = sb("cnt_i", [P, E], I32)
        tiles_f = sb("tiles_f", [P, E])
        tiles_inc = sb("tiles_inc", [P, E])
        posn = sb("posn", [P, E, GB])
        prod = sb("prod", [P, GB, E])
        dest_f = sb("dest_f", [P, 2, GB])
        dest_i = sb("dest_i", [P, GROUPS, 2, GB], I32)
        tcmp = sb("tcmp", [P, GT, E])
        texp = sb("texp", [P, GT])
        tile_expert = sb("tile_expert", [P, TILES], I32)

        xs = sb("xs", [P, 4, RC])
        exT = sb("exT", [P, 2, P])
        silu = sb("silu", [P, 2, H])
        hid = sb("hid", [P, 2, H])
        hidT = sb("hidT", [P, 2, 2, P])
        ys = sb("ys", [P, 4, D])
        yb = sb("yb", [P, 4, TOPK, D])

        sorted_rows = nc.dram_tensor("sorted_rows", (TILES * P, RC), F32, kind="Internal").ap()
        expert_out = nc.dram_tensor("expert_out", (B * T * TOPK, D), F32, kind="Internal").ap()

        bank = [stack.enter_context(nc.psum_tensor(f"bank{i}", [P, 512], F32)) for i in range(8)]
        BK_XT, BK_KQ, BK_MAX, BK_SC, BK_PV, BK_TAIL = 0, 1, 2, 4, 6, 7

        ld_x = [sem(f"ld_x{i}") for i in range(4)]
        ld_w = sem("ld_w")
        ld_con = sem("ld_con")
        ld_small = sem("ld_small")
        ld_bias = sem("ld_bias")
        ld_mask = sem("ld_mask")
        ld_ew = sem("ld_ew")
        ld_ctx = [sem(f"ld_ctx{i}") for i in range(4)]
        blanked = sem("blanked")
        blank_ready = sem("blank_ready")
        bias_rows = sem("bias_rows")
        waits_over = sem("waits_over")
        su = sem("setup_vector")
        sg = sem("setup_gpsimd")
        pe_a, pe_b, pe_c, pe_d0, pe_d1, pe_e = (sem(f"pe_{k}") for k in (
            "xn_transposed", "kq", "v", "max0", "max1", "shift_transposed"))
        pe_f0, pe_f1, pe_g, pe_h, pe_i, pe_j, pe_k = (sem(f"pe_{k}") for k in (
            "scores0", "scores1", "weighted", "upd_transposed", "proj", "x2_transposed", "logits"))
        act_exp0, act_exp1, act_xnT, act_x2T, act_updT, act_v = (sem(f"act_{k}") for k in (
            "exp0", "exp1", "xnT", "x2T", "updT", "v"))
        dve_bn1, dve_agg1, dve_xn, dve_max, dve_mh, dve_mneg, dve_mT = (sem(f"dve_{k}") for k in (
            "bn1", "agg1", "xn", "max", "shift_high", "shift", "mT"))
        dve_k, dve_q, dve_rs, dve_upd, dve_x1, dve_bn2, dve_agg2, dve_x2n, dve_logit = (
            sem(f"dve_{k}") for k in ("k", "q", "rsum", "upd", "x1", "bn2", "agg2", "x2n", "logit"))
        pool_v1, pool_rs1, pool_v2, pool_rs2, pool_q, pool_rows = (sem(f"pool_{k}") for k in (
            "var1", "rstd1", "var2", "rstd2", "q", "rows"))
        route = sem("route_step")
        gap_ready, gexp_ready = sem("gap_ready"), sem("gexp_ready")
        counts_in, counted, counts_read, routed = (sem(k) for k in ("counts_in", "counted", "counts_read", "routed"))
        sent = [sem(f"rows_sent{g}") for g in range(GROUPS)]
        ld_xs = [sem(f"ld_tile{i}") for i in range(4)]
        y_sent = [sem(f"y_sent{i}") for i in range(4)]
        pe_T, pe_H, pe_A, pe_Y = (sem(f"pe_{k}") for k in ("tile_transposed", "hidden", "hid_transposed", "y"))
        act_exT, act_silu = sem("act_exT"), sem("act_silu")
        dve_hid, dve_hidT, dve_y = sem("dve_hid"), sem("dve_hidT"), sem("dve_y")
        ld_yb = [sem(f"ld_yb{i}") for i in range(4)]
        dve_y0, dve_out, st_out = sem("dve_y0"), sem("dve_out"), sem("st_out")

        block = stack.enter_context(nc.Block())

        def attention_steps(step, between=None):
            for n in range(-4, 4):
                step(n, n % U)
            yield (4, 20)
            if between:
                between(0)
            yield (20, 28)
            for n in range(28, B + 3):
                step(n, n % U)
            if between:
                between(1)

        def loop_steps(engine, step, lo, hi):
            with engine.Fori(lo // U, hi // U) as q:
                base = engine.snap(q * U)
                for u in range(U):
                    step(base + u, u)

        def run_attention(engine, step, between=None):
            for lo, hi in attention_steps(step, between):
                loop_steps(engine, step, lo, hi)

        @block.sync
        def _(sp):
            sp.dma_start(xres[:, 0:8, :], x[0:8].rearrange("b t d -> t b d")).then_inc(ld_x[0], 16)
            sp.dma_start(con[:], consts).then_inc(ld_con, 16)
            sp.dma_start(wat[:], w_attn).then_inc(ld_w, 16)

            def step(n, u):
                b = n + 4
                if live(b):
                    need(sp, pe_c, b - 3)
                    sp.dma_start(ctx[:, u], ctxT[bass.ds(b, 1)].rearrange("b p c s -> p (b c) s")).then_inc(
                        ld_ctx[u], 16)

            for n in range(-4, 0):
                step(n, n % U)
            for i in range(1, 4):
                sp.dma_start(xres[:, 8 * i:8 * i + 8, :],
                             x[8 * i:8 * i + 8].rearrange("b t d -> t b d")).then_inc(ld_x[i], 16)
            for n in range(0, 4):
                step(n, n % U)
            sp.dma_start(w01s[:], w01).then_inc(ld_ew, 16)
            sp.dma_start(w2s[:], w2).then_inc(ld_ew, 16)
            loop_steps(sp, step, 4, B - 4)

            def load_tile(i, r, q):
                need(sp, y_sent[r], 16 * q)
                sp.dma_start(xs[:, r, :], sorted_rows[bass.ds(i * P, P), :]).then_inc(ld_xs[r], 16)

            sp.wait_ge(sent[0], 16 * TOPK * GB)
            sp.wait_ge(blanked, 16)
            for i in range(4):
                load_tile(i, i, 0)
            with sp.Fori(1, 9) as q:
                for r in range(4):
                    load_tile(q * 4 + r, r, q)
            sp.wait_ge(sent[1], 16 * TOPK * GB)
            with sp.Fori(9, TILES // 4) as q:
                for r in range(4):
                    load_tile(q * 4 + r, r, q)
            for i in range(TILES // 4 * 4, TILES):
                load_tile(i, i % 4, i // 4)

            for r in range(4):
                sp.wait_ge(y_sent[r], 16 * len(range(r, TILES, 4)))
            pairs = expert_out.rearrange("(b t k) d -> t b (k d)", b=B, k=TOPK)
            for b in range(4):
                sp.dma_start(yb[:, b].rearrange("p k d -> p (k d)"), pairs[:, b, :]).then_inc(ld_yb[b], 16)
            with sp.Fori(1, B // 4) as q:
                base = sp.snap(q * 4)
                for u in range(4):
                    sp.wait_ge(dve_out, base + (u - 3))
                    sp.dma_start(yb[:, u].rearrange("p k d -> p (k d)"),
                                 pairs[:, bass.ds(base + u, 1), :].rearrange("t b c -> t (b c)")).then_inc(ld_yb[u], 16)

        @block.scalar
        def _(act):
            act.dma_start(colsb[:], cols).then_inc(ld_small, 16)
            act.dma_start(gbias[:], gate_b.partition_broadcast(P)).then_inc(ld_small, 16)
            act.dma_start(idsb[:], ids).then_inc(ld_small, 16)
            act.dma_start(bias_f[:], biases).then_inc(ld_bias, 16)
            act.dma_start(maskr[:], mask_row.partition_broadcast(P)).then_inc(ld_mask, 16)
            act.wait_ge(su, 5)
            act.wait_ge(sg, 5)
            for k in range(3):
                act.dma_start(bias3[k:k + 1, :], bias_p[:, k, :]).then_inc(bias_rows, 16)
            act.wait_ge(blank_ready, 2)
            act.dma_start(sorted_rows.rearrange("(i p) c -> p i c", p=P),
                          blank[:].rearrange("p (i c) -> p i c", i=1).to_broadcast([P, TILES, RC])).then_inc(blanked, 16)
            act.wait_ge(su, 9)

            def step(n, u):
                if live(n):
                    p = u % 2
                    for half, (scored, done) in enumerate(((pe_f0, act_exp0), (pe_f1, act_exp1))):
                        need(act, scored, n + 1)
                        need(act, pe_g, n - 1)
                        stand(act, waits_over)
                        nc.scalar.activation(
                            attn[:, p, HALF * half:HALF * half + HALF, :],
                            bank[BK_SC + half][:].rearrange("p (h t) -> p h t", h=HALF), ACT.Exp,
                            bias=keyb[:, bass.ds(n, 1)], scale=HD ** -0.5).then_inc(done, 1)
                        if half == 0:
                            transposed(n, u)
                else:
                    transposed(n, u)
                if live(n - 1):
                    p = (u - 1) % 2
                    need(act, pe_h, n)
                    need(act, pe_i, n - 2)
                    nc.scalar.copy(updT[:, p, :], bank[BK_TAIL][:, 0:T]).then_inc(act_updT, 1)
                if live(n + 1):
                    p = (u + 1) % 2
                    need(act, pe_c, n + 2)
                    need(act, pe_g, n)
                    stand(act, waits_over)
                    nc.scalar.activation(vaug[:, p, :, 0:HD],
                                         bank[BK_PV][:, 0:D].rearrange("p (h d) -> p h d", h=HEADS),
                                         ACT.Identity, scale=colsb[:, bass.ds(n + 3, 1)]).then_inc(act_v, 1)

            def transposed(n, u):
                if live(n + 2):
                    r = (u + 2) % 4
                    need(act, pe_a, n + 3)
                    need(act, pe_i, n - 1)
                    nc.scalar.copy(xnT[:, r, :], bank[BK_XT][:, 0:T]).then_inc(act_xnT, 1)
                if live(n - 2):
                    p = u % 2
                    need(act, pe_j, n - 1)
                    need(act, pe_k, n - 3)
                    nc.scalar.copy(x2T[:, p, :], bank[BK_TAIL][:, 0:T]).then_inc(act_x2T, 1)

            def between(g):
                act.wait_ge(gap_ready, g + 1)
                nc.scalar.activation(gexp[:], gap[:], ACT.Exp).then_inc(gexp_ready, 1)

            run_attention(act, step, between)

            def tile_T(i, p):
                need(act, pe_T, i + 1)
                need(act, pe_H, i - 1)
                nc.scalar.copy(exT[:, p, :], bank[BK_XT][:, 0:P]).then_inc(act_exT, 1)

            def tile_silu(i, p):
                need(act, pe_H, i + 1)
                need(act, dve_hid, i - 1)
                nc.scalar.activation(silu[:, p, :], bank[BK_MAX + p][:, H:2 * H], ACT.Silu).then_inc(act_silu, 1)

            tile_T(0, 0)
            tile_T(1, 1)
            for i in range(2):
                tile_silu(i, i)
                tile_T(i + 2, i)
            with act.Fori(1, TILES // 2 - 1) as q:
                base = act.snap(q * 2)
                for p in range(2):
                    tile_silu(base + p, p)
                    tile_T(base + (p + 2), p)
            for i in range(TILES - 2, TILES):
                tile_silu(i, i % 2)

            with act.Fori(0, B) as b:
                act.wait_ge(dve_out, b + 1)
                act.dma_start(out[bass.ds(b, 1)].rearrange("b t d -> t (b d)"),
                              xres[:, bass.ds(b, 1), :].rearrange("p b d -> p (b d)")).then_inc(st_out, 16)
            act.wait_ge(st_out, 16 * B)

        @block.gpsimd
        def _(pool):
            nc.gpsimd.memset(blank[:], 0.0).then_inc(blank_ready, 1)
            pool.wait_ge(blank_ready, 1)
            nc.gpsimd.memset(blank[:, D:D + 1].bitcast(I32), NOWHERE).then_inc(blank_ready, 1)
            nc.gpsimd.memset(bias3[:], 0.0).then_inc(sg, 1)
            nc.gpsimd.memset(mhalf[:], -0.5).then_inc(sg, 1)
            nc.gpsimd.memset(ones_b[:], 1.0).then_inc(sg, 1)
            nc.gpsimd.memset(mneg[:], 0.0).then_inc(sg, 1)
            nc.gpsimd.memset(vaug[:], 1.0).then_inc(sg, 1)
            nc.gpsimd.memset(onesf[:], 1.0).then_inc(sg, 1)
            pool.wait_ge(sg, 6)
            pool.wait_ge(ld_con, 16)
            pool.wait_ge(su, 8)

            def rstd(done, v, o, agg, mv, ve, rs, c, r):
                need(pool, agg, c)
                stand(pool, waits_over)
                nc.gpsimd.tensor_scalar(ve[:, r:r + 1], mv[:, r, 1:2], EPS, None, ALU.add).then_inc(v, 1)
                need(pool, v, c)
                nc.gpsimd.tensor_tensor(rs[:, r:r + 1], ve[:, r:r + 1], mhalf[:], ALU.pow).then_inc(done, 1)

            patt = con[:, C_PATT:C_PATT + HALF].rearrange("p (j o) -> p j o", o=1).to_broadcast([P, HALF, T])

            def step(n, u):
                if live(n + 2):
                    p = u % 2
                    need(pool, pe_d1, n + 1)
                    stand(pool, waits_over)
                    nc.gpsimd.tensor_copy(mb[:, p, :], maskb[:, bass.ds((n + 2) * T, T)])
                    need(pool, dve_k, n + 3)
                    stand(pool, waits_over)
                    nc.gpsimd.tensor_copy(kb[:, p, :], kf[:, p, :])
                    need(pool, dve_q, n + 3)
                    qb = qf[:, p, :].rearrange("p (o t) -> p o t", o=1).to_broadcast([P, HALF, T])
                    nc.gpsimd.tensor_tensor(q4b[:, p], qb, patt, ALU.mult)
                    need(pool, pe_f1, n + 1)
                    nc.gpsimd.tensor_tensor(q4[:, p], qb, patt, ALU.mult).then_inc(pool_q, 1)
                if live(n - 1):
                    need(pool, dve_x2n, n - 4)
                    rstd(pool_rs2, pool_v2, None, dve_agg2, mv2, ve2, rs2, n, (u - 1) % 4)
                if live(n + 4):
                    need(pool, dve_xn, n + 1)
                    rstd(pool_rs1, pool_v1, None, dve_agg1, mv1, ve1, rs1, n + 5, u)
                if live(n - 1):
                    p = (u - 1) % 2
                    need(pool, dve_x2n, n)
                    src = x2n[:, p, :].rearrange("p (o d) -> p o d", o=1).to_broadcast([P, TOPK, D])
                    nc.gpsimd.tensor_copy(rows[:, bass.ds(n - 1, 1), :, 0:D].rearrange("p b k d -> p (b k) d"),
                                          src).then_inc(pool_rows, 1)

            def send(g, b):
                for k in range(TOPK):
                    nc.gpsimd.indirect_dma_start(
                        out=sorted_rows,
                        out_offset=bass.IndirectOffsetOnAxis(ap=dest_i[:, g, k, b - g * GB:b - g * GB + 1], axis=0),
                        in_=rows[:, b, k, :], in_offset=None,
                        bounds_check=TILES * P - 1, oob_is_err=False).then_inc(sent[g], 16)

            for n in range(-4, 4):
                step(n, n % U)
            loop_steps(pool, step, 4, 20)
            for n in range(20, B + 3):
                step(n, n % U)
                if n == 20:
                    pool.wait_ge(blanked, 16)
                    pool.wait_ge(routed, 1)
                for b in range(2 * (n - 20), min(2 * (n - 20) + 2, GB)):
                    send(0, b)
            pool.wait_ge(routed, 2)
            for b in range(GB, B):
                send(1, b)

            def send_y(i, r):
                need(pool, dve_y, i + 1)
                stand(pool, waits_over)
                nc.gpsimd.indirect_dma_start(
                    out=expert_out,
                    out_offset=bass.IndirectOffsetOnAxis(ap=xs[:, r, D:D + 1].bitcast(I32), axis=0),
                    in_=ys[:, r, :], in_offset=None,
                    bounds_check=B * T * TOPK - 1, oob_is_err=False).then_inc(y_sent[r], 16)

            with pool.Fori(0, TILES // 4) as q:
                base = pool.snap(q * 4)
                for r in range(4):
                    send_y(base + r, r)
            for i in range(TILES // 4 * 4, TILES):
                send_y(i, i % 4)

        @block.vector
        def _(dve):
            dve.wait_ge(ld_bias, 16)
            nc.vector.tensor_copy(bias_p[:, 0, :], bias_f[:]).then_inc(su, 1)
            dve.wait_ge(su, 1)
            nc.vector.tensor_tensor(bias_r[:, 0, :], bias_f[:], bias_p[:, 0, :], ALU.subtract).then_inc(su, 1)
            dve.wait_ge(su, 2)
            nc.vector.tensor_copy(bias_p[:, 1, :], bias_r[:, 0, :]).then_inc(su, 1)
            dve.wait_ge(su, 3)
            nc.vector.tensor_tensor(bias_r[:, 1, :], bias_r[:, 0, :], bias_p[:, 1, :], ALU.subtract).then_inc(su, 1)
            dve.wait_ge(su, 4)
            nc.vector.tensor_copy(bias_p[:, 2, :], bias_r[:, 1, :]).then_inc(su, 1)
            dve.wait_ge(ld_con, 16)
            nc.vector.tensor_copy(ident_b[:], con[:, C_IDENT:C_IDENT + P])
            nc.vector.tensor_copy(tri_b[:], con[:, C_TRI:C_TRI + P])
            nc.vector.tensor_copy(row0_b[:], con[:, C_ROW0:C_ROW0 + 1].to_broadcast([P, P])).then_inc(su, 1)
            nc.vector.tensor_copy(sel_b[:], con[:, C_SEL:C_SEL + 4].rearrange("p (j o) -> p j o", o=1).to_broadcast(
                [P, 4, P])).then_inc(su, 1)
            dve.wait_ge(ld_mask, 16)
            nc.vector.tensor_scalar(maskb[:], maskr[:], 0.0, FAR, ALU.is_equal, ALU.mult).then_inc(su, 1)
            dve.wait_ge(ld_small, 48)
            nc.vector.tensor_scalar(keyb[:], colsb[:, 2:2 + B], 0.0, FAR, ALU.is_equal, ALU.mult).then_inc(su, 1)
            dve.wait_ge(sg, 6)
            nc.vector.tensor_copy(rows[:, :, :, D:D + 1].rearrange("p b k o -> p (b k o)").bitcast(I32), idsb[:])

            def stats(b, u, bn, agg, st, mv, used):
                stand(dve, waits_over)
                nc.vector.bn_stats(st[:, u % 2, :], xres[:, bass.ds(b, 1), :].rearrange("p b d -> p (b d)")).then_inc(bn, 1)
                need(dve, bn, b + 1)
                need(dve, used, b - 3)
                stand(dve, waits_over)
                nc.vector.bn_aggr(mv[:, u % 4, :], st[:, u % 2, :]).then_inc(agg, 1)

            def normalise(o, b, u, mv, rs):
                nc.vector.tensor_scalar(o, xres[:, bass.ds(b, 1), :].rearrange("p b d -> p (b d)"),
                                        mv[:, u % 4, 0:1], rs[:, u % 4:u % 4 + 1], ALU.subtract, ALU.mult)

            def step(n, u):
                if live(n - 2):
                    need(dve, pe_k, n - 1)
                    nc.vector.tensor_tensor(logits[:, bass.ds(n - 2, 1), :].rearrange("p b e -> p (b e)"),
                                            bank[BK_TAIL][:, 0:E], gbias[:], ALU.add).then_inc(dve_logit, 1)
                if live(n + 3):
                    b, v = n + 3, (u + 3) % 4
                    need(dve, pool_rs1, b + 1)
                    need(dve, pe_a, b - 1)
                    nc.vector.tensor_scalar(xn[:, v % 2, :], xres[:, bass.ds(b, 1), :].rearrange("p b d -> p (b d)"),
                                            mv1[:, v, 0:1], rs1[:, v:v + 1], ALU.subtract, ALU.mult).then_inc(dve_xn, 1)
                if live(n + 1):
                    b, p = n + 1, (u + 1) % 2
                    for half, scored in enumerate((pe_d0, pe_d1)):
                        need(dve, scored, b + 1)
                        last = nc.vector.tensor_reduce(nmax[:, p, HALF * half:HALF * half + HALF],
                                                       bank[BK_MAX + half][:].rearrange("p (h s) -> p h s", h=HALF),
                                                       AX_X, ALU.max, negate=True)
                    last.then_inc(dve_max, 1)
                    need(dve, dve_max, b + 1)
                    need(dve, pe_e, b - 1)
                    nm = nmax[:, p, :].rearrange("p (a j) -> p a j", a=2)
                    parts = mneg[:, p, :].rearrange("p (a q j) -> p a q j", a=2, j=HALF)
                    nc.vector.tensor_copy(parts[:, :, 0, :], nm).then_inc(dve_mh, 1)
                    need(dve, dve_mh, b + 1)
                    nc.vector.tensor_tensor(parts[:, :, 1, :], nm, parts[:, :, 0, :], ALU.subtract).then_inc(dve_mneg, 1)
                if live(n - 1):
                    b, v = n - 1, (u - 1) % 4
                    need(dve, pe_i, b + 1)
                    xb = xres[:, bass.ds(b, 1), :].rearrange("p b d -> p (b d)")
                    nc.vector.tensor_tensor(xb, bank[BK_TAIL][:, 0:D], xb, ALU.add).then_inc(dve_x1, 1)
                    need(dve, dve_x1, b + 1)
                    stats(b, v, dve_bn2, dve_agg2, st2, mv2, pool_rs2)
                if live(n + 2):
                    b, p = n + 2, u % 2
                    need(dve, pe_b, b + 1)
                    need(dve, pe_f1, b - 1)
                    need(dve, pool_q, b - 1)
                    mrow = maskr[:, bass.ds(b * T, T)]
                    nc.vector.scalar_tensor_tensor(kf[:, p, :], bank[BK_KQ][:, 0:T], colsb[:, 0:1], mrow,
                                                   ALU.add, ALU.mult).then_inc(dve_k, 1)
                    nc.vector.scalar_tensor_tensor(qf[:, p, :], bank[BK_KQ][:, T:2 * T], colsb[:, 1:2], mrow,
                                                   ALU.add, ALU.mult).then_inc(dve_q, 1)
                if live(n + 4):
                    stats(n + 4, u, dve_bn1, dve_agg1, st1, mv1, pool_rs1)
                if live(n):
                    b, p = n, u % 2
                    need(dve, pe_g, b + 1)
                    pv = bank[BK_PV][:, 0:HEADS * (HD + 1)].rearrange("p (h d) -> p h d", h=HEADS)
                    nc.vector.reciprocal(rsum[:, p, :], pv[:, :, HD]).then_inc(dve_rs, 1)
                    need(dve, dve_rs, b + 1)
                    need(dve, pe_h, b - 1)
                    nc.vector.tensor_tensor(upd[:, p, :].rearrange("p (h d) -> p h d", h=HEADS), pv[:, :, 0:HD],
                                            rsum[:, p, :].rearrange("p (h o) -> p h o", o=1).to_broadcast(
                                                [P, HEADS, HD]), ALU.mult).then_inc(dve_upd, 1)
                if live(n - 1):
                    b, v = n - 1, (u - 1) % 4
                    need(dve, pool_rs2, b + 1)
                    need(dve, pe_j, b - 1)
                    need(dve, pool_rows, b - 1)
                    nc.vector.tensor_scalar(x2n[:, v % 2, :], xres[:, bass.ds(b, 1), :].rearrange("p b d -> p (b d)"),
                                            mv2[:, v, 0:1], rs2[:, v:v + 1], ALU.subtract, ALU.mult).then_inc(dve_x2n, 1)
                if live(n + 1):
                    b, p = n + 1, (u + 1) % 2
                    need(dve, pe_e, b + 1)
                    need(dve, pe_f1, b - 1)
                    nc.vector.tensor_copy(mT[:, p, :], bank[BK_TAIL][:].bitcast(BF16)[:, 0:T]).then_inc(dve_mT, 1)

            steps = [0]

            def link(instruction):
                steps[0] += 1
                instruction.then_inc(route, 1)
                dve.wait_ge(route, steps[0])

            def wide(ap, shape, where):
                return ap.rearrange(where, o=1).to_broadcast(shape)

            def between(g):
                dve.wait_ge(dve_logit, GB * (g + 1))
                dve.wait_ge(pool_rows, GB * (g + 1))
                lg = logits[:, GB * g:GB * g + GB, :]
                rev = con[:, C_REV:C_REV + E].rearrange("p (o e) -> p o e", o=1).to_broadcast([P, GB, E])
                src = lg
                for k in range(TOPK):
                    link(nc.vector.tensor_reduce(top[:, k, :], src, AX_X, ALU.max))
                    link(nc.vector.tensor_tensor(eqs[:], src, wide(top[:, k, :], [P, GB, E], "p (b o) -> p b o"),
                                                 ALU.is_equal))
                    link(nc.vector.tensor_tensor(eqs[:], eqs[:], rev, ALU.mult))
                    link(nc.vector.tensor_reduce(first[:, k, :], eqs[:], AX_X, ALU.max))
                    link(nc.vector.tensor_tensor(hot[:, k], wide(first[:, k, :], [P, GB, E], "p (b o) -> p b o"),
                                                 rev, ALU.is_equal))
                    if k == 0:
                        link(nc.vector.scalar_tensor_tensor(lower[:], hot[:, 0], -3.0e38, lg, ALU.mult, ALU.add))
                        src = lower[:]
                nc.vector.tensor_tensor(gap[:], top[:, 1, :], top[:, 0, :], ALU.subtract).then_inc(gap_ready, 1)
                link(nc.vector.tensor_tensor(picked[:].rearrange("p e b -> p b e"), hot[:, 0], hot[:, 1], ALU.add))
                pk = picked[:].rearrange("p e b -> p (e b)")
                link(nc.vector.tensor_tensor_scan(running[:], onesf[:, 0:E * GB], pk, 0.0, ALU.mult, ALU.add))
                link(nc.vector.tensor_reduce(rowsum[:], picked[:], AX_X, ALU.add))
                nc.vector.tensor_copy(rowsum_b[:], rowsum[:]).then_inc(counts_in, 1)
                link(nc.vector.tensor_tensor_scan(rowinc[:], onesf[:, 0:E], rowsum[:], 0.0, ALU.mult, ALU.add))
                dve.wait_ge(counted, g + 1)
                nc.vector.tensor_copy(counts[:], bank[BK_XT][:, 0:2 * E]).then_inc(counts_read, 1)
                dve.wait_ge(counts_read, g + 1)
                link(nc.vector.tensor_scalar(tiles_f[:], counts[:, E:2 * E], float(P - 1), None, ALU.add))
                link(nc.vector.tensor_copy(cnt_i[:], tiles_f[:]))
                link(nc.vector.tensor_scalar(cnt_i[:], cnt_i[:], 7, None, ALU.logical_shift_right))
                link(nc.vector.tensor_copy(tiles_f[:], cnt_i[:]))
                link(nc.vector.tensor_tensor_scan(tiles_inc[:], onesf[:, 0:E], tiles_f[:], 0.0, ALU.mult, ALU.add))
                link(nc.vector.tensor_tensor(place[:], tiles_inc[:], tiles_f[:], ALU.subtract))
                link(nc.vector.scalar_tensor_tensor(place[:], place[:], float(P), counts[:, 0:E], ALU.mult, ALU.add))
                link(nc.vector.tensor_tensor(place[:], place[:], rowinc[:], ALU.subtract))
                link(nc.vector.tensor_tensor(place[:], place[:], rowsum[:], ALU.add))
                link(nc.vector.tensor_tensor(posn[:].rearrange("p e b -> p (e b)"), running[:], pk, ALU.subtract))
                link(nc.vector.tensor_tensor(posn[:], posn[:], wide(place[:], [P, E, GB], "p (e o) -> p e o"), ALU.add))
                for k in range(TOPK):
                    link(nc.vector.tensor_tensor(prod[:], hot[:, k], posn[:].rearrange("p e b -> p b e"), ALU.mult))
                    link(nc.vector.tensor_reduce(dest_f[:, k, :], prod[:], AX_X, ALU.add))
                link(nc.vector.tensor_scalar(dest_i[:, g], dest_f[:], float(g * GT * P), None, ALU.add))
                link(nc.vector.tensor_tensor(
                    tcmp[:], tiles_inc[:].rearrange("p (o e) -> p o e", o=1).to_broadcast([P, GT, E]),
                    wide(con[:, C_TILE:C_TILE + GT], [P, GT, E], "p (i o) -> p i o"), ALU.is_le))
                link(nc.vector.tensor_reduce(texp[:], tcmp[:], AX_X, ALU.add))
                link(nc.vector.tensor_scalar(tile_expert[:, GT * g:GT * g + GT], texp[:], float(E - 1), None, ALU.min))
                dve.wait_ge(gexp_ready, g + 1)
                link(nc.vector.tensor_scalar(gden[:], gexp[:], 1.0, None, ALU.add))
                weight = rows[:, GB * g:GB * g + GB, :, D + 1]
                link(nc.vector.reciprocal(weight[:, :, 0], gden[:]))
                nc.vector.tensor_tensor(weight[:, :, 1], gexp[:], weight[:, :, 0], ALU.mult).then_inc(routed, 1)

            dve.wait_ge(ld_x[0], 16)
            for n in range(-4, 4):
                step(n, n % U)
            for i in range(1, 4):
                dve.wait_ge(ld_x[i], 16)
            loop_steps(dve, step, 4, 20)
            between(0)
            loop_steps(dve, step, 20, 28)
            for n in range(28, B + 3):
                step(n, n % U)
            between(1)

            def tile_hidT(i, p):
                need(dve, pe_A, i + 1)
                need(dve, pe_Y, i - 1)
                nc.vector.tensor_copy(hidT[:, p], bank[BK_KQ][:, 0:2 * P].rearrange("p (c t) -> p c t", c=2)).then_inc(
                    dve_hidT, 1)

            def tile_y(i, r, q):
                need(dve, pe_Y, i + 1)
                need(dve, y_sent[r], 16 * q)
                nc.vector.tensor_scalar(ys[:, r, :], bank[BK_PV][:, 0:D], xs[:, r, D + 1:D + 2], None,
                                        ALU.mult).then_inc(dve_y, 1)

            def tile_hid(i, p):
                need(dve, act_silu, i + 1)
                need(dve, pe_A, i - 1)
                nc.vector.tensor_tensor(hid[:, p, :], bank[BK_MAX + p][:, 0:H], silu[:, p, :], ALU.mult).then_inc(
                    dve_hid, 1)

            def tile_step(i, r, q, qy):
                if not isinstance(i, int) or i >= 2:
                    tile_hidT(i - 2, r % 2)
                    tile_y(i - 2, (r - 2) % 4, qy)
                if not isinstance(i, int) or i < TILES:
                    tile_hid(i, r % 2)

            for i in range(4):
                tile_step(i, i, 0, 0)
            with dve.Fori(1, TILES // 4) as q:
                for r in range(4):
                    tile_step(q * 4 + r, r, q, q - 1 if r < 2 else q)
            for i in range(TILES // 4 * 4, TILES + 2):
                tile_step(i, i % 4, i // 4, (i - 2) // 4)

            def combine(b, r, q):
                dve.wait_ge(ld_yb[r], 16 * (q + 1))
                xb = xres[:, bass.ds(b, 1), :].rearrange("p b d -> p (b d)")
                nc.vector.tensor_tensor(xb, xb, yb[:, r, 0, :], ALU.add).then_inc(dve_y0, 1)
                dve.wait_ge(dve_y0, b + 1)
                nc.vector.tensor_tensor(xb, xb, yb[:, r, 1, :], ALU.add).then_inc(dve_out, 1)

            with dve.Fori(0, B // 4) as q:
                for r in range(4):
                    combine(q * 4 + r, r, q)

        @block.tensor
        def _(pe):
            ident = con[:, C_IDENT:C_IDENT + P]
            pe.wait_ge(ld_con, 16)
            pe.wait_ge(ld_w, 16)
            pe.wait_ge(bias_rows, 48)
            pe.wait_ge(sg, 6)
            pe.wait_ge(su, 7)

            def mm(o, lhsT, rhs, start=True, stop=True):
                return nc.tensor.matmul(o, lhsT, rhs, start=start, stop=stop)

            def step(n, u):
                if live(n):
                    scores(n, u, 0)
                if live(n + 2):
                    b, p = n + 2, u % 2
                    need(pe, dve_xn, b + 1)
                    need(pe, act_xnT, b)
                    nc.tensor.transpose(bank[BK_XT][:, 0:T], xn[:, p, :], ident).then_inc(pe_a, 1)
                if live(n - 2):
                    b, p = n - 2, u % 2
                    need(pe, dve_x2n, b + 1)
                    need(pe, dve_mT, upto(b + 3))
                    nc.tensor.transpose(bank[BK_TAIL][:, 0:T], x2n[:, p, :], ident).then_inc(pe_j, 1)
                if live(n):
                    scores(n, u, 1)
                if live(n - 2):
                    b, p = n - 2, u % 2
                    need(pe, act_x2T, b + 1)
                    mm(bank[BK_TAIL][:, 0:E], x2T[:, p, :], wat[:, WG:WG + E]).then_inc(pe_k, 1)
                if live(n + 1):
                    b, p = n + 1, (u + 1) % 2
                    need(pe, pool_q, b + 1)
                    need(pe, dve_max, b)
                    for half, done in enumerate((pe_d0, pe_d1)):
                        s = slice(64 * half, 64 * half + 64)
                        dst = bank[BK_MAX + half]
                        mm(dst[:].rearrange("p (h s) -> p h s", h=HALF), row0_b[s, :],
                           mb[s, p, :].rearrange("p (o s) -> p o s", o=1).to_broadcast([64, HALF, T]), stop=False)
                        for j in range(HALF):
                            last = mm(dst[:, j * T:j * T + T], q4b[s, p, j, :], kb[s, p, :], start=False,
                                      stop=j == HALF - 1)
                        last.then_inc(done, 1)
                if live(n - 1):
                    b, p = n - 1, (u - 1) % 2
                    need(pe, dve_upd, b + 1)
                    need(pe, dve_logit, b)
                    nc.tensor.transpose(bank[BK_TAIL][:, 0:T], upd[:, p, :], ident).then_inc(pe_h, 1)
                if live(n + 1):
                    b, r = n + 1, (u + 1) % 4
                    need(pe, dve_upd, b - 1)
                    if isinstance(b, int) and b == 1:
                        pe.wait_ge(act_v, 1)
                    dst = bank[BK_PV][:, 0:D]
                    for c in range(2):
                        mm(dst, ctx[:, r, c, :], wat[:, WV + D * c:WV + D * c + D], start=c == 0, stop=False)
                    mm(dst, ones_b[:], bias3[:, BV:BV + D], start=False).then_inc(pe_c, 1)
                if live(n - 1):
                    b, p, r = n - 1, (u - 1) % 2, (u - 1) % 4
                    dst = bank[BK_TAIL][:, 0:D]
                    need(pe, act_updT, b + 1)
                    mm(dst, xnT[:, r, :], wat[:, WO:WO + D], stop=False)
                    mm(dst, updT[:, p, :], wat[:, WO + D:WO + 2 * D], start=False, stop=False)
                    mm(dst, ones_b[:], bias3[:, BO:BO + D], start=False).then_inc(pe_i, 1)
                if live(n + 2):
                    b, r = n + 2, (u + 2) % 4
                    need(pe, ld_ctx[r], ctx_loads(n, u + 2))
                    need(pe, act_xnT, b + 1)
                    need(pe, dve_q, b)
                    for c in range(2):
                        mm(bank[BK_KQ][:, 0:T], wat[:, WK + D * c:WK + D * c + D], ctx[:, r, c, :], start=c == 0,
                           stop=c == 1)
                    mm(bank[BK_KQ][:, T:2 * T], wat[:, WQ:WQ + D], xnT[:, r, :]).then_inc(pe_b, 1)
                if live(n):
                    b, p = n, u % 2
                    need(pe, act_v, upto(b + 2))
                    for h in range(HEADS):
                        if h == 0:
                            need(pe, act_exp0, b + 1)
                        if h == HALF:
                            need(pe, act_exp1, b + 1)
                        last = mm(bank[BK_PV][:, h * (HD + 1):(h + 1) * (HD + 1)], attn[:, p, h, :], vaug[:, p, h, :])
                    last.then_inc(pe_g, 1)
                if live(n + 1):
                    b, p = n + 1, (u + 1) % 2
                    need(pe, dve_mneg, b + 1)
                    need(pe, dve_x1, b - 1)
                    nc.tensor.transpose(bank[BK_TAIL][:].bitcast(BF16)[:, 0:T], mneg[:, p, :], ident_b[:]).then_inc(
                        pe_e, 1)

            def ctx_loads(n, v):
                if isinstance(n, int):
                    return 16 * ((n + 2) // 4 + 1)
                return (n + (2 + 4 - v % 4)) * 4

            def scores(n, u, half):
                p = u % 2
                s = slice(64 * half, 64 * half + 64)
                dst = bank[BK_SC + half]
                if half == 0:
                    need(pe, dve_mT, n + 1)
                need(pe, (act_exp0, act_exp1)[half], n)
                mm(dst[:].rearrange("p (h t) -> p h t", h=HALF), kf[s, p, :], q4[s, p], stop=False)
                for j in range(HALF):
                    last = mm(dst[:, j * T:j * T + T], sel_b[s, j, :], mT[s, p, :], start=False, stop=j == HALF - 1)
                last.then_inc((pe_f0, pe_f1)[half], 1)

            def between(g):
                pe.wait_ge(counts_in, g + 1)
                if g == 0:
                    pe.wait_ge(act_xnT, 22)
                mm(bank[BK_XT][:, 0:E], tri_b[:], rowsum_b[:])
                mm(bank[BK_XT][:, E:2 * E], ones_b[:], rowsum_b[:]).then_inc(counted, 1)
                pe.wait_ge(counts_read, g + 1)

            run_attention(pe, step, between)

            def expert(i):
                return pe.value_load(tile_expert[0:1, bass.ds(i, 1)], min_val=0, max_val=E - 1)

            def tile_T(i, r, q):
                need(pe, ld_xs[r], (q + 1) * 16)
                need(pe, act_exT, i)
                nc.tensor.transpose(bank[BK_XT][:, 0:P], xs[:, r, 0:D], ident).then_inc(pe_T, 1)

            def tile_H(i, p, e):
                need(pe, act_exT, i + 1)
                need(pe, dve_hid, i - 1)
                dst = bank[BK_MAX + p][:]
                mm(dst, exT[:, p, :], w01s[:, bass.ds(e * (2 * H), 2 * H)], stop=False)
                mm(dst, ones_b[:], bias3[:, bass.ds(e * (2 * H) + B01, 2 * H)], start=False).then_inc(pe_H, 1)

            def tile_A(i, p):
                need(pe, dve_hid, i + 1)
                need(pe, dve_hidT, i)
                for c in range(2):
                    last = nc.tensor.transpose(bank[BK_KQ][:, c * P:c * P + P], hid[:, p, c * P:c * P + P], ident)
                last.then_inc(pe_A, 1)

            def tile_Y(i, p, e):
                need(pe, dve_hidT, i + 1)
                need(pe, dve_y, i)
                dst = bank[BK_PV][:, 0:D]
                for c in range(2):
                    mm(dst, hidT[:, p, c, :], w2s[:, bass.ds(e * (2 * D) + c * D, D)], start=c == 0, stop=False)
                mm(dst, ones_b[:], bias3[:, bass.ds(e * D + B2, D)], start=False).then_inc(pe_Y, 1)

            def tile_step(i, r, q, ahead=True):
                static = isinstance(i, int)
                if not static or i >= 2:
                    tile_A(i - 2, r % 2)
                if not static or i < TILES:
                    tile_H(i, r % 2, expert(i))
                if not static or i >= 2:
                    tile_Y(i - 2, r % 2, expert(i - 2))
                if not static or i + 2 < TILES:
                    tile_T(i + 2, (r + 2) % 4, q if r < 2 else q + 1)

            pe.wait_ge(ld_ew, 32)
            pe.wait_ge(routed, 2)
            tile_T(0, 0, 0)
            tile_T(1, 1, 0)
            for i in range(4):
                tile_step(i, i, 0)
            with pe.Fori(1, TILES // 4) as q:
                for r in range(4):
                    tile_step(q * 4 + r, r, q)
            for i in range(TILES // 4 * 4, TILES + 2):
                tile_step(i, i % 4, i // 4)


def kernel(**inputs):
    import numpy as np
    import concourse.bacc as bacc
    from concourse.bass_utils import run_bass_kernel_spmd

    def get(name):
        return np.asarray(inputs[name])

    def c(a):
        return np.ascontiguousarray(a)

    x, context, mask = get("x"), get("ctx_2048"), get("mask_BxS2_fk1")
    w_src, w_tgt, w_out = get("L0_xattn_W_src"), get("L0_xattn_W_tgt"), get("L0_xattn_W_out")
    b_src = get("L0_xattn_b_src")
    ctxT = c(context.transpose(0, 2, 1).reshape(B, 2, P, T).transpose(0, 2, 1, 3))
    wkT, wvT = w_src[:D].T.reshape(2, P, D), w_src[D:].T.reshape(2, P, D)
    woT = w_out.T.reshape(2, P, D)
    w_attn = c(np.concatenate([wkT[0], wkT[1], wvT[0], wvT[1], w_tgt.T, woT[0], woT[1], get("L0_ffn_gate_w").T], 1))
    cols = c(np.concatenate([b_src[:D, None], get("L0_xattn_b_tgt")[:, None], mask.T], 1))
    biases = c(np.concatenate([b_src[D:], get("L0_xattn_b_out"),
                               np.concatenate([get("L0_ffn_b0"), get("L0_ffn_b1")], 1).reshape(-1),
                               get("L0_ffn_b2").reshape(-1)]).reshape(P, BIASES // P))
    w01 = c(np.concatenate([get("L0_ffn_w0"), get("L0_ffn_w1")], 1).transpose(2, 0, 1).reshape(P, E * 2 * H))
    w2 = c(get("L0_ffn_w2").reshape(E, D, 2, P).transpose(3, 0, 2, 1).reshape(P, E * 2 * D))
    p = np.arange(P)
    consts = np.zeros((P, C_COLS), np.float32)
    consts[:, C_IDENT:C_IDENT + P] = np.eye(P)
    consts[:, C_TRI:C_TRI + P] = p[:, None] < p[None, :]
    consts[:, C_PATT:C_PATT + HALF] = (p % 64 // HD)[:, None] == np.arange(HALF)[None, :]
    consts[:, C_SEL:C_SEL + 4] = (p % 4)[:, None] == np.arange(4)[None, :]
    consts[:, C_ROW0] = p % 64 == 0
    consts[:, C_REV:C_REV + E] = E - np.arange(E)[None, :]
    consts[:, C_TILE:C_TILE + GT] = np.arange(GT)[None, :]
    token = (np.arange(B)[None, :, None] * T + p[:, None, None]) * TOPK + np.arange(TOPK)[None, None, :]
    arrays = {
        "x": c(x), "ctxT": ctxT, "w_attn": w_attn, "cols": cols, "mask_row": c(mask.reshape(1, -1)[0]),
        "gate_b": c(get("L0_ffn_gate_b")), "biases": biases, "w01": w01, "w2": w2, "consts": consts,
        "ids": c(token.reshape(P, B * TOPK).astype(np.int32)),
    }
    nc = bacc.Bacc("TRN2", target_bir_lowering=False, num_devices=1)
    handles = {k: nc.dram_tensor(k, v.shape, mybir.dt.from_np(v.dtype), kind="ExternalInput").ap()
               for k, v in arrays.items()}
    out = nc.dram_tensor("out", (B, T, D), F32, kind="ExternalOutput").ap()
    build(nc, *handles.values(), out)
    r = run_bass_kernel_spmd(nc, [arrays], core_ids=[0])
    return r.results[0]["out"]
```

```python
from contextlib import ExitStack

import concourse.bass as bass
from concourse import mybir

F32 = mybir.dt.float32
BF16 = mybir.dt.bfloat16
I32 = mybir.dt.int32
ALU = mybir.AluOpType
ACT = mybir.ActivationFunctionType
AX_X = mybir.AxisListType.X

P = 128
B, T, D, DS = 32, 128, 128, 256
HEADS, HD = 8, 16
HALF = HEADS // 2
E, H, TOPK = 8, 256, 2
EPS = 1e-5
FAR = -1.0e30
GROUPS = 2
GB = B // GROUPS
GT = GB * T * TOPK // P + E - 1
TILES = GROUPS * GT
RC = D + 2
NOWHERE = 1 << 20
U = 4
R = 8
ROUTE = GB + U
COMBINE = 7
assert GB == 2 * R and GT < (COMBINE - 1) * R and COMBINE * R + GB < TILES
assert ROUTE % U == 0 and B % U == 0

WK, WV, WQ, WO, WG = 0, 2 * D, 4 * D, 5 * D, 7 * D
W_COLS = 7 * D + E
C_IDENT, C_TRI, C_PATT, C_SEL = 0, P, 2 * P, 2 * P + HALF
C_ROW0, C_REV, C_TILE = C_SEL + HEADS, C_SEL + HEADS + 1, C_SEL + HEADS + 1 + E
C_COLS = C_TILE + GT
BV, BO, B01, B2 = 0, D, 2 * D, 2 * D + E * 2 * H
BIASES = B2 + E * D


def need(engine, sem, count):
    if not isinstance(count, int) or count > 0:
        engine.wait_ge(sem, count)


def live(b):
    return not isinstance(b, int) or 0 <= b < B


def stand(engine, waits_over):
    engine.sem_inc(waits_over, 1)


def upto(count):
    return min(count, B) if isinstance(count, int) else count


def build(nc, x, ctxT, w_attn, cols, mask_row, gate_b, biases, w01, w2, consts, ids, out):
    with ExitStack() as stack:
        def sb(name, shape, dt=F32):
            return stack.enter_context(nc.sbuf_tensor(name, shape, dt))

        def sem(name):
            return stack.enter_context(nc.semaphore(name))

        xres = sb("xres", [P, B, D])
        rows = sb("rows", [P, B, TOPK, RC])
        ctx = sb("ctx", [P, 4, 2, T])
        wat = sb("wat", [P, W_COLS])
        w01s = sb("w01s", [P, E * 2 * H])
        w2s = sb("w2s", [P, E * 2 * D])
        bias3 = sb("bias3", [P, BIASES], BF16)
        bias_f = sb("bias_f", [P, BIASES // P])
        bias_r = sb("bias_r", [P, 2, BIASES // P])
        bias_p = sb("bias_p", [P, 3, BIASES // P], BF16)
        colsb = sb("colsb", [P, 2 + B])
        maskr = sb("maskr", [P, B * T])
        maskb = sb("maskb", [P, B * T], BF16)
        keyb = sb("keyb", [P, B])
        gbias = sb("gbias", [P, E])
        con = sb("con", [P, C_COLS])
        idsb = sb("idsb", [P, B * TOPK], I32)
        ident_b = sb("ident_b", [P, P], BF16)
        tri_b = sb("tri_b", [P, P], BF16)
        ones_b = sb("ones_b", [P, P], BF16)
        row0_b = sb("row0_b", [P, P], BF16)
        sel_b = sb("sel_b", [P, HEADS, P], BF16)
        onesf = sb("onesf", [P, P])
        mhalf = sb("mhalf", [P, 1])
        blank = sb("blank", [P, RC])

        st1 = sb("st1", [P, 2, 6])
        mv1 = sb("mv1", [P, 4, 2])
        ve1 = sb("ve1", [P, 4])
        rs1 = sb("rs1", [P, 4])
        st2 = sb("st2", [P, 2, 6])
        mv2 = sb("mv2", [P, 4, 2])
        ve2 = sb("ve2", [P, 4])
        rs2 = sb("rs2", [P, 4])
        xn = sb("xn", [P, 2, D])
        xnT = sb("xnT", [P, 4, T])
        kz = sb("kz", [P, 2, 2, T])
        headmask = sb("headmask", [P, 2, HALF, T])
        kb = sb("kb", [P, 2, 2, T], BF16)
        q4 = sb("q4", [P, 2, HALF, T])
        q4b = sb("q4b", [P, 2, HALF, T], BF16)
        nmax = sb("nmax", [P, 2, HEADS])
        mneg = sb("mneg", [P, 2, P], BF16)
        mT = sb("mT", [P, 2, T], BF16)
        attn = sb("attn", [P, 2, HEADS, T])
        vaug = sb("vaug", [P, 2, HEADS, HD + 1])
        rsum = sb("rsum", [P, 2, HEADS])
        upd = sb("upd", [P, 2, D])
        updT = sb("updT", [P, 2, T])
        x2n = sb("x2n", [P, 2, D])
        x2T = sb("x2T", [P, 2, T])
        logits = sb("logits", [P, B, E])

        top = sb("top", [P, 2, GB])
        first = sb("first", [P, 2, GB])
        eqs = sb("eqs", [P, GB, E])
        hot = sb("hot", [P, 2, GB, E])
        lower = sb("lower", [P, GB, E])
        gap = sb("gap", [P, GB])
        gexp = sb("gexp", [P, GB])
        gden = sb("gden", [P, GB])
        picked = sb("picked", [P, E, GB])
        running = sb("running", [P, E * GB])
        rowsum = sb("rowsum", [P, E])
        rowsum_b = sb("rowsum_b", [P, E], BF16)
        rowinc = sb("rowinc", [P, E])
        counts = sb("counts", [P, 2 * E])
        place = sb("place", [P, E])
        cnt_i = sb("cnt_i", [P, E], I32)
        tiles_f = sb("tiles_f", [P, E])
        tiles_inc = sb("tiles_inc", [P, E])
        posn = sb("posn", [P, E, GB])
        prod = sb("prod", [P, GB, E])
        dest_f = sb("dest_f", [P, 2, GB])
        dest_i = sb("dest_i", [P, GROUPS, 2, GB], I32)
        tcmp = sb("tcmp", [P, GT, E])
        texp = sb("texp", [P, GT])
        tile_expert = sb("tile_expert", [P, TILES], I32)

        xs = sb("xs", [P, R, RC])
        exT = sb("exT", [P, 2, P])
        silu = sb("silu", [P, 2, H])
        hid = sb("hid", [P, 2, H])
        hidT = sb("hidT", [P, 2, 2, P])
        ys = sb("ys", [P, R, D])
        yb = sb("yb", [P, R, TOPK, D])

        sorted_rows = nc.dram_tensor("sorted_rows", (TILES * P, RC), F32, kind="Internal").ap()
        expert_out = nc.dram_tensor("expert_out", (B * T * TOPK, D), F32, kind="Internal").ap()

        bank = [stack.enter_context(nc.psum_tensor(f"bank{i}", [P, 512], F32)) for i in range(8)]
        BK_XT, BK_KQ, BK_MAX, BK_SC, BK_PV, BK_TAIL = 0, 1, 2, 4, 6, 7

        ld_x = [sem(f"ld_x{i}") for i in range(4)]
        ld_w = sem("ld_w")
        ld_con = sem("ld_con")
        ld_small = sem("ld_small")
        ld_bias = sem("ld_bias")
        ld_mask = sem("ld_mask")
        ld_ew = sem("ld_ew")
        ld_ctx = [sem(f"ld_ctx{i}") for i in range(4)]
        blanked = sem("blanked")
        blank_ready = sem("blank_ready")
        bias_rows = sem("bias_rows")
        waits_over = sem("waits_over")
        su = sem("setup_vector")
        sg = sem("setup_gpsimd")
        pe_a, pe_b, pe_c, pe_d0, pe_d1, pe_e = (sem(f"pe_{k}") for k in (
            "xn_transposed", "kq", "v", "max0", "max1", "shift_transposed"))
        pe_f0, pe_f1, pe_g, pe_h, pe_i, pe_j, pe_k = (sem(f"pe_{k}") for k in (
            "scores0", "scores1", "weighted", "upd_transposed", "proj", "x2_transposed", "logits"))
        act_exp0, act_exp1, act_xnT, act_x2T, act_updT, act_v = (sem(f"act_{k}") for k in (
            "exp0", "exp1", "xnT", "x2T", "updT", "v"))
        dve_bn1, dve_agg1, dve_xn, dve_max, dve_mh, dve_mneg, dve_mT = (sem(f"dve_{k}") for k in (
            "bn1", "agg1", "xn", "max", "shift_high", "shift", "mT"))
        dve_k, dve_q, dve_rs, dve_upd, dve_x1, dve_bn2, dve_agg2, dve_x2n, dve_logit = (
            sem(f"dve_{k}") for k in ("k", "q", "rsum", "upd", "x1", "bn2", "agg2", "x2n", "logit"))
        pool_v1, pool_rs1, pool_v2, pool_rs2, pool_hm = (sem(f"pool_{k}") for k in (
            "var1", "rstd1", "var2", "rstd2", "headmask"))
        act_kq, act_rows = sem("act_kq_bf16"), sem("act_rows")
        route = sem("route_step")
        gap_ready, gexp_ready = sem("gap_ready"), sem("gexp_ready")
        counts_in, counted, counts_read, routed = (sem(k) for k in ("counts_in", "counted", "counts_read", "routed"))
        sent = [sem(f"rows_sent{g}") for g in range(GROUPS)]
        ld_xs = [sem(f"ld_tile{i}") for i in range(R)]
        y_sent = [sem(f"y_sent{i}") for i in range(R)]
        pe_T, pe_H, pe_A, pe_Y = (sem(f"pe_{k}") for k in ("tile_transposed", "hidden", "hid_transposed", "y"))
        act_exT, act_silu = sem("act_exT"), sem("act_silu")
        dve_hid, dve_hidT, dve_y = sem("dve_hid"), sem("dve_hidT"), sem("dve_y")
        ld_yb = [sem(f"ld_yb{i}") for i in range(R)]
        dve_y0, dve_out, st_out = sem("dve_y0"), sem("dve_out"), sem("st_out")

        block = stack.enter_context(nc.Block())

        def loop_steps(engine, step, lo, hi):
            with engine.Fori(lo // U, hi // U) as q:
                base = engine.snap(q * U)
                for u in range(U):
                    step(base + u, u)

        def run_attention(engine, step, after=None):
            for n in range(-4, U):
                step(n, n % U)
            loop_steps(engine, step, U, ROUTE)
            for n in range(ROUTE, ROUTE + U):
                step(n, n % U)
                if after:
                    after(n)
            loop_steps(engine, step, ROUTE + U, B - U)
            for n in range(B - U, B + 3):
                step(n, n % U)

        @block.sync
        def _(sp):
            sp.dma_start(xres[:, 0:8, :], x[0:8].rearrange("b t d -> t b d")).then_inc(ld_x[0], 16)
            sp.dma_start(con[:], consts).then_inc(ld_con, 16)
            sp.dma_start(wat[:], w_attn).then_inc(ld_w, 16)

            def step(n, u):
                b = n + 4
                if live(b):
                    need(sp, pe_c, b - 3)
                    sp.dma_start(ctx[:, u], ctxT[bass.ds(b, 1)].rearrange("b p c s -> p (b c) s")).then_inc(
                        ld_ctx[u], 16)

            for n in range(-4, 0):
                step(n, n % U)
            for i in range(1, 4):
                sp.dma_start(xres[:, 8 * i:8 * i + 8, :],
                             x[8 * i:8 * i + 8].rearrange("b t d -> t b d")).then_inc(ld_x[i], 16)
            for n in range(0, 4):
                step(n, n % U)
            sp.dma_start(w01s[:], w01).then_inc(ld_ew, 16)
            sp.dma_start(w2s[:], w2).then_inc(ld_ew, 16)
            loop_steps(sp, step, 4, B - 4)

            def load_tile(i, r, q):
                need(sp, y_sent[r], 16 * q)
                sp.dma_start(xs[:, r, :], sorted_rows[bass.ds(i * P, P), :]).then_inc(ld_xs[r], 16)

            pairs = expert_out.rearrange("(b t k) d -> b t (k d)", b=B, k=TOPK)

            def load_pair(b, r):
                need(sp, dve_out, b - (R - 1))
                sp.dma_start(yb[:, r].rearrange("p k d -> p (k d)"),
                             pairs[bass.ds(b, 1)].rearrange("b t c -> (b t) c")).then_inc(ld_yb[r], 16)

            sp.wait_ge(sent[0], 16 * TOPK * GB)
            sp.wait_ge(blanked, 16)
            for i in range(R):
                load_tile(i, i, 0)
            with sp.Fori(1, GT // R) as q:
                for r in range(R):
                    load_tile(q * R + r, r, q)
            sp.wait_ge(sent[1], 16 * TOPK * GB)
            with sp.Fori(GT // R, COMBINE) as q:
                for r in range(R):
                    load_tile(q * R + r, r, q)
            for r in range(R):
                sp.wait_ge(y_sent[r], 16 * len(range(r, GT, R)))
            for i in range(COMBINE * R, COMBINE * R + GB):
                load_tile(i, i % R, i // R)
                load_pair(i - COMBINE * R, i % R)
            for i in range(COMBINE * R + GB, TILES):
                load_tile(i, i % R, i // R)
            for r in range(R):
                sp.wait_ge(y_sent[r], 16 * len(range(r, TILES, R)))
            for b in range(GB, B):
                load_pair(b, b % R)

        @block.scalar
        def _(act):
            act.dma_start(colsb[:], cols).then_inc(ld_small, 16)
            act.dma_start(gbias[:], gate_b.partition_broadcast(P)).then_inc(ld_small, 16)
            act.dma_start(idsb[:], ids).then_inc(ld_small, 16)
            act.dma_start(bias_f[:], biases).then_inc(ld_bias, 16)
            act.dma_start(maskr[:], mask_row.partition_broadcast(P)).then_inc(ld_mask, 16)
            act.wait_ge(su, 5)
            act.wait_ge(sg, 5)
            for k in range(3):
                act.dma_start(bias3[k:k + 1, :], bias_p[:, k, :]).then_inc(bias_rows, 16)
            act.wait_ge(blank_ready, 2)
            act.dma_start(sorted_rows.rearrange("(i p) c -> p i c", p=P),
                          blank[:].rearrange("p (i c) -> p i c", i=1).to_broadcast([P, TILES, RC])).then_inc(blanked, 16)
            act.wait_ge(su, 9)

            def step(n, u):
                if live(n):
                    p = u % 2
                    for half, (scored, done) in enumerate(((pe_f0, act_exp0), (pe_f1, act_exp1))):
                        need(act, scored, n + 1)
                        need(act, pe_g, n - 1)
                        stand(act, waits_over)
                        nc.scalar.activation(
                            attn[:, p, HALF * half:HALF * half + HALF, :],
                            bank[BK_SC + half][:].rearrange("p (h t) -> p h t", h=HALF), ACT.Exp,
                            bias=keyb[:, bass.ds(n, 1)], scale=HD ** -0.5).then_inc(done, 1)
                        if half == 0:
                            transposed(n, u)
                else:
                    transposed(n, u)
                if live(n - 2):
                    p = u % 2
                    need(act, dve_x2n, n - 1)
                    src = x2n[:, p, :].rearrange("p (o d) -> p o d", o=1).to_broadcast([P, TOPK, D])
                    nc.scalar.copy(rows[:, bass.ds(n - 2, 1), :, 0:D].rearrange("p b k d -> p (b k) d"),
                                   src).then_inc(act_rows, 1)
                if live(n - 1):
                    p = (u - 1) % 2
                    need(act, pe_h, n)
                    need(act, pe_i, n - 2)
                    nc.scalar.copy(updT[:, p, :], bank[BK_TAIL][:, 0:T]).then_inc(act_updT, 1)
                if live(n + 1):
                    p = (u + 1) % 2
                    need(act, pe_c, n + 2)
                    need(act, pe_g, n)
                    stand(act, waits_over)
                    nc.scalar.activation(vaug[:, p, :, 0:HD],
                                         bank[BK_PV][:, 0:D].rearrange("p (h d) -> p h d", h=HEADS),
                                         ACT.Identity, scale=colsb[:, bass.ds(n + 3, 1)]).then_inc(act_v, 1)
                if live(n + 2):
                    p = u % 2
                    need(act, pe_d1, n + 1)
                    need(act, dve_k, n + 3)
                    nc.scalar.copy(kb[:, p], kz[:, p])
                    need(act, dve_q, n + 3)
                    nc.scalar.copy(q4b[:, p], q4[:, p]).then_inc(act_kq, 1)

            def transposed(n, u):
                if live(n + 2):
                    r = (u + 2) % 4
                    need(act, pe_a, n + 3)
                    need(act, pe_i, n - 1)
                    nc.scalar.copy(xnT[:, r, :], bank[BK_XT][:, 0:T]).then_inc(act_xnT, 1)
                if live(n - 2):
                    p = u % 2
                    need(act, pe_j, n - 1)
                    need(act, pe_k, n - 3)
                    nc.scalar.copy(x2T[:, p, :], bank[BK_TAIL][:, 0:T]).then_inc(act_x2T, 1)

            def weigh(g):
                act.wait_ge(gap_ready, g + 1)
                nc.scalar.activation(gexp[:], gap[:], ACT.Exp).then_inc(gexp_ready, 1)

            def after(n):
                if n == ROUTE + 2:
                    weigh(0)

            run_attention(act, step, after)

            def tile_T(i, p):
                need(act, pe_T, i + 1)
                need(act, pe_H, i - 1)
                nc.scalar.copy(exT[:, p, :], bank[BK_XT][:, 0:P]).then_inc(act_exT, 1)

            def tile_silu(i, p):
                need(act, pe_H, i + 1)
                need(act, dve_hid, i - 1)
                nc.scalar.activation(silu[:, p, :], bank[BK_MAX + p][:, H:2 * H], ACT.Silu).then_inc(act_silu, 1)

            def store(b):
                act.wait_ge(dve_out, b + 1)
                act.dma_start(out[b], xres[:, b, :]).then_inc(st_out, 16)

            tile_T(0, 0)
            tile_T(1, 1)
            weigh(1)
            for i in range(2):
                tile_silu(i, i)
                tile_T(i + 2, i)
            with act.Fori(1, COMBINE * R // 2) as q:
                base = act.snap(q * 2)
                for p in range(2):
                    tile_silu(base + p, p)
                    tile_T(base + (p + 2), p)
            for i in range(COMBINE * R, TILES):
                tile_silu(i, i % 2)
                if i + 2 < TILES:
                    tile_T(i + 2, i % 2)
                b = i - COMBINE * R - 2
                if 0 <= b < GB:
                    store(b)
            for b in range(GB, B):
                store(b)
            act.wait_ge(st_out, 16 * B)

        @block.gpsimd
        def _(pool):
            nc.gpsimd.memset(blank[:], 0.0).then_inc(blank_ready, 1)
            pool.wait_ge(blank_ready, 1)
            nc.gpsimd.memset(blank[:, D:D + 1].bitcast(I32), NOWHERE).then_inc(blank_ready, 1)
            nc.gpsimd.memset(bias3[:], 0.0).then_inc(sg, 1)
            nc.gpsimd.memset(mhalf[:], -0.5).then_inc(sg, 1)
            nc.gpsimd.memset(ones_b[:], 1.0).then_inc(sg, 1)
            nc.gpsimd.memset(mneg[:], 0.0).then_inc(sg, 1)
            nc.gpsimd.memset(vaug[:], 1.0).then_inc(sg, 1)
            nc.gpsimd.memset(onesf[:], 1.0).then_inc(sg, 1)
            nc.gpsimd.memset(kz[:], 0.0).then_inc(sg, 1)
            pool.wait_ge(sg, 7)
            pool.wait_ge(ld_con, 16)
            pool.wait_ge(su, 8)

            def rstd(done, v, agg, mv, ve, rs, c, r):
                need(pool, agg, c)
                stand(pool, waits_over)
                nc.gpsimd.tensor_scalar(ve[:, r:r + 1], mv[:, r, 1:2], EPS, None, ALU.add).then_inc(v, 1)
                need(pool, v, c)
                nc.gpsimd.tensor_tensor(rs[:, r:r + 1], ve[:, r:r + 1], mhalf[:], ALU.pow).then_inc(done, 1)

            patt = con[:, C_PATT:C_PATT + HALF].rearrange("p (j o) -> p j o", o=1).to_broadcast([P, HALF, T])

            def step(n, u):
                if live(n + 4):
                    need(pool, dve_xn, n + 1)
                    rstd(pool_rs1, pool_v1, dve_agg1, mv1, ve1, rs1, n + 5, u)
                if live(n + 3):
                    need(pool, dve_q, n + 2)
                    stand(pool, waits_over)
                    mrow = maskr[:, bass.ds((n + 3) * T, T)].rearrange("p (o t) -> p o t", o=1)
                    nc.gpsimd.tensor_tensor(headmask[:, (u + 1) % 2], mrow.to_broadcast([P, HALF, T]), patt,
                                            ALU.mult).then_inc(pool_hm, 1)
                if live(n - 1):
                    need(pool, dve_x2n, n - 4)
                    rstd(pool_rs2, pool_v2, dve_agg2, mv2, ve2, rs2, n, (u - 1) % 4)

            def send(g, b):
                for k in range(TOPK):
                    nc.gpsimd.indirect_dma_start(
                        out=sorted_rows,
                        out_offset=bass.IndirectOffsetOnAxis(ap=dest_i[:, g, k, b - g * GB:b - g * GB + 1], axis=0),
                        in_=rows[:, b, k, :], in_offset=None,
                        bounds_check=TILES * P - 1, oob_is_err=False).then_inc(sent[g], 16)

            for n in range(-4, U):
                step(n, n % U)
            loop_steps(pool, step, U, ROUTE + U)
            waiting = list(range(GB))
            for n in range(ROUTE + U, B + 3):
                step(n, n % U)
                if n == ROUTE + U:
                    pool.wait_ge(blanked, 16)
                    pool.wait_ge(routed, 1)
                    pool.wait_ge(act_rows, GB)
                for b in waiting[:2]:
                    send(0, b)
                waiting = waiting[2:]
            pool.wait_ge(routed, 2)
            pool.wait_ge(act_rows, B)
            for b in range(GB, B):
                send(1, b)

            def send_y(i, r):
                need(pool, dve_y, i + 1)
                stand(pool, waits_over)
                nc.gpsimd.indirect_dma_start(
                    out=expert_out,
                    out_offset=bass.IndirectOffsetOnAxis(ap=xs[:, r, D:D + 1].bitcast(I32), axis=0),
                    in_=ys[:, r, :], in_offset=None,
                    bounds_check=B * T * TOPK - 1, oob_is_err=False).then_inc(y_sent[r], 16)

            with pool.Fori(0, TILES // R) as q:
                base = pool.snap(q * R)
                for r in range(R):
                    send_y(base + r, r)
            for i in range(TILES // R * R, TILES):
                send_y(i, i % R)

        @block.vector
        def _(dve):
            dve.wait_ge(ld_bias, 16)
            nc.vector.tensor_copy(bias_p[:, 0, :], bias_f[:]).then_inc(su, 1)
            dve.wait_ge(su, 1)
            nc.vector.tensor_tensor(bias_r[:, 0, :], bias_f[:], bias_p[:, 0, :], ALU.subtract).then_inc(su, 1)
            dve.wait_ge(su, 2)
            nc.vector.tensor_copy(bias_p[:, 1, :], bias_r[:, 0, :]).then_inc(su, 1)
            dve.wait_ge(su, 3)
            nc.vector.tensor_tensor(bias_r[:, 1, :], bias_r[:, 0, :], bias_p[:, 1, :], ALU.subtract).then_inc(su, 1)
            dve.wait_ge(su, 4)
            nc.vector.tensor_copy(bias_p[:, 2, :], bias_r[:, 1, :]).then_inc(su, 1)
            dve.wait_ge(ld_con, 16)
            nc.vector.tensor_copy(ident_b[:], con[:, C_IDENT:C_IDENT + P])
            nc.vector.tensor_copy(tri_b[:], con[:, C_TRI:C_TRI + P])
            nc.vector.tensor_copy(row0_b[:], con[:, C_ROW0:C_ROW0 + 1].to_broadcast([P, P])).then_inc(su, 1)
            nc.vector.tensor_copy(sel_b[:], con[:, C_SEL:C_SEL + HEADS].rearrange("p (j o) -> p j o", o=1).to_broadcast(
                [P, HEADS, P])).then_inc(su, 1)
            dve.wait_ge(ld_mask, 16)
            nc.vector.tensor_scalar(maskb[:], maskr[:], 0.0, FAR, ALU.is_equal, ALU.mult).then_inc(su, 1)
            dve.wait_ge(ld_small, 48)
            nc.vector.tensor_scalar(keyb[:], colsb[:, 2:2 + B], 0.0, FAR, ALU.is_equal, ALU.mult).then_inc(su, 1)
            dve.wait_ge(sg, 7)
            nc.vector.tensor_copy(rows[:, :, :, D:D + 1].rearrange("p b k o -> p (b k o)").bitcast(I32), idsb[:])

            def batch(b):
                return xres[:, bass.ds(b, 1), :].rearrange("p b d -> p (b d)")

            def stats(b, v, bn, st):
                stand(dve, waits_over)
                nc.vector.bn_stats(st[:, v % 2, :], batch(b)).then_inc(bn, 1)

            def aggregate(b, v, bn, agg, st, mv, used):
                need(dve, bn, b + 1)
                need(dve, used, b - 3)
                stand(dve, waits_over)
                nc.vector.bn_aggr(mv[:, v, :], st[:, v % 2, :]).then_inc(agg, 1)

            def step(n, u):
                s_1, s1, s2, s3, s4 = ((u + k) % 4 for k in (-1, 1, 2, 3, 4))
                p, p1, p2 = u % 2, (u + 1) % 2, u % 2
                nm = nmax[:, p1, :].rearrange("p (a j) -> p a j", a=2)
                parts = mneg[:, p1, :].rearrange("p (a q j) -> p a q j", a=2, j=HALF)
                if live(n + 3):
                    need(dve, pool_rs1, n + 4)
                    need(dve, pe_a, n + 2)
                    nc.vector.tensor_scalar(xn[:, p1, :], batch(n + 3), mv1[:, s3, 0:1], rs1[:, s3:s3 + 1],
                                            ALU.subtract, ALU.mult).then_inc(dve_xn, 1)
                if live(n + 4):
                    stats(n + 4, s4, dve_bn1, st1)
                if live(n - 2):
                    need(dve, pe_k, n - 1)
                    nc.vector.tensor_tensor(logits[:, bass.ds(n - 2, 1), :].rearrange("p b e -> p (b e)"),
                                            bank[BK_TAIL][:, 0:E], gbias[:], ALU.add).then_inc(dve_logit, 1)
                if live(n + 1):
                    for half, scored in enumerate((pe_d0, pe_d1)):
                        need(dve, scored, n + 2)
                        last = nc.vector.tensor_reduce(nmax[:, p1, HALF * half:HALF * half + HALF],
                                                       bank[BK_MAX + half][:].rearrange("p (h s) -> p h s", h=HALF),
                                                       AX_X, ALU.max, negate=True)
                    last.then_inc(dve_max, 1)
                if live(n + 4):
                    aggregate(n + 4, s4, dve_bn1, dve_agg1, st1, mv1, pool_rs1)
                if live(n + 1):
                    need(dve, dve_max, n + 2)
                    need(dve, pe_e, n)
                    nc.vector.tensor_copy(parts[:, :, 0, :], nm).then_inc(dve_mh, 1)
                if live(n - 1):
                    need(dve, pe_i, n)
                    nc.vector.tensor_tensor(batch(n - 1), bank[BK_TAIL][:, 0:D], batch(n - 1), ALU.add).then_inc(
                        dve_x1, 1)
                if live(n + 1):
                    need(dve, dve_mh, n + 2)
                    nc.vector.tensor_tensor(parts[:, :, 1, :], nm, parts[:, :, 0, :], ALU.subtract).then_inc(dve_mneg, 1)
                if live(n - 1):
                    need(dve, dve_x1, n)
                    stats(n - 1, s_1, dve_bn2, st2)
                if live(n - 1):
                    aggregate(n - 1, s_1, dve_bn2, dve_agg2, st2, mv2, pool_rs2)
                if live(n + 1):
                    need(dve, pe_e, n + 2)
                    need(dve, pe_f1, n)
                    nc.vector.tensor_copy(mT[:, p1, :], bank[BK_TAIL][:].bitcast(BF16)[:, 0:T]).then_inc(dve_mT, 1)
                if live(n + 2):
                    need(dve, pe_b, n + 3)
                    need(dve, pe_f1, n + 1)
                    need(dve, act_kq, n + 1)
                    for half in range(2):
                        s = slice(64 * half, 64 * half + 64)
                        last = nc.vector.scalar_tensor_tensor(
                            kz[s, p2, half, :], bank[BK_KQ][s, 0:T], colsb[s, 0:1],
                            maskr[s, bass.ds((n + 2) * T, T)], ALU.add, ALU.mult)
                    last.then_inc(dve_k, 1)
                    need(dve, pool_hm, n + 3)
                    q = bank[BK_KQ][:, T:2 * T].rearrange("p (o t) -> p o t", o=1).to_broadcast([P, HALF, T])
                    nc.vector.scalar_tensor_tensor(q4[:, p2], q, colsb[:, 1:2], headmask[:, p2], ALU.add,
                                                   ALU.mult).then_inc(dve_q, 1)
                if live(n - 1):
                    need(dve, pool_rs2, n)
                    need(dve, pe_j, n - 2)
                    need(dve, act_rows, n - 2)
                    nc.vector.tensor_scalar(x2n[:, p1, :], batch(n - 1), mv2[:, s_1, 0:1], rs2[:, s_1:s_1 + 1],
                                            ALU.subtract, ALU.mult).then_inc(dve_x2n, 1)
                pv = bank[BK_PV][:, 0:HEADS * (HD + 1)].rearrange("p (h d) -> p h d", h=HEADS)
                if live(n):
                    need(dve, pe_g, n + 1)
                    nc.vector.reciprocal(rsum[:, p, :], pv[:, :, HD]).then_inc(dve_rs, 1)
                    need(dve, dve_rs, n + 1)
                    need(dve, pe_h, n - 1)
                    nc.vector.tensor_tensor(upd[:, p, :].rearrange("p (h d) -> p h d", h=HEADS), pv[:, :, 0:HD],
                                            rsum[:, p, :].rearrange("p (h o) -> p h o", o=1).to_broadcast(
                                                [P, HEADS, HD]), ALU.mult).then_inc(dve_upd, 1)

            steps = [0]

            def link(instruction):
                steps[0] += 1
                instruction.then_inc(route, 1)
                dve.wait_ge(route, steps[0])

            def wide(ap, shape, where):
                return ap.rearrange(where, o=1).to_broadcast(shape)

            rev = con[:, C_REV:C_REV + E].rearrange("p (o e) -> p o e", o=1).to_broadcast([P, GB, E])
            pk = picked[:].rearrange("p e b -> p (e b)")

            def choose(g, k):
                src = lower[:] if k else logits[:, GB * g:GB * g + GB, :]
                if k == 0:
                    dve.wait_ge(dve_logit, GB * (g + 1))
                link(nc.vector.tensor_reduce(top[:, k, :], src, AX_X, ALU.max))
                link(nc.vector.tensor_tensor(eqs[:], src, wide(top[:, k, :], [P, GB, E], "p (b o) -> p b o"),
                                             ALU.is_equal))
                link(nc.vector.tensor_tensor(eqs[:], eqs[:], rev, ALU.mult))
                link(nc.vector.tensor_reduce(first[:, k, :], eqs[:], AX_X, ALU.max))
                link(nc.vector.tensor_tensor(hot[:, k], wide(first[:, k, :], [P, GB, E], "p (b o) -> p b o"),
                                             rev, ALU.is_equal))
                if k == 0:
                    link(nc.vector.scalar_tensor_tensor(lower[:], hot[:, 0], -3.0e38, src, ALU.mult, ALU.add))

            def count(g):
                nc.vector.tensor_tensor(gap[:], top[:, 1, :], top[:, 0, :], ALU.subtract).then_inc(gap_ready, 1)
                link(nc.vector.tensor_tensor(picked[:].rearrange("p e b -> p b e"), hot[:, 0], hot[:, 1], ALU.add))
                link(nc.vector.tensor_reduce(rowsum[:], picked[:], AX_X, ALU.add))
                nc.vector.tensor_copy(rowsum_b[:], rowsum[:]).then_inc(counts_in, 1)
                link(nc.vector.tensor_tensor_scan(running[:], onesf[:, 0:E * GB], pk, 0.0, ALU.mult, ALU.add))
                link(nc.vector.tensor_tensor_scan(rowinc[:], onesf[:, 0:E], rowsum[:], 0.0, ALU.mult, ALU.add))

            def read_counts(g, src):
                dve.wait_ge(counted, g + 1)
                nc.vector.tensor_copy(counts[:], src[:, 0:2 * E]).then_inc(counts_read, 1)
                dve.wait_ge(counts_read, g + 1)
                link(nc.vector.tensor_scalar(tiles_f[:], counts[:, E:2 * E], float(P - 1), None, ALU.add))
                link(nc.vector.tensor_copy(cnt_i[:], tiles_f[:]))
                link(nc.vector.tensor_scalar(cnt_i[:], cnt_i[:], P.bit_length() - 1, None, ALU.logical_shift_right))
                link(nc.vector.tensor_copy(tiles_f[:], cnt_i[:]))
                link(nc.vector.tensor_tensor_scan(tiles_inc[:], onesf[:, 0:E], tiles_f[:], 0.0, ALU.mult, ALU.add))
                link(nc.vector.tensor_tensor(place[:], tiles_inc[:], tiles_f[:], ALU.subtract))
                link(nc.vector.scalar_tensor_tensor(place[:], place[:], float(P), counts[:, 0:E], ALU.mult, ALU.add))
                link(nc.vector.tensor_tensor(place[:], place[:], rowinc[:], ALU.subtract))
                link(nc.vector.tensor_tensor(place[:], place[:], rowsum[:], ALU.add))

            def route_rows(g):
                link(nc.vector.tensor_tensor(posn[:].rearrange("p e b -> p (e b)"), running[:], pk, ALU.subtract))
                link(nc.vector.tensor_tensor(posn[:], posn[:], wide(place[:], [P, E, GB], "p (e o) -> p e o"), ALU.add))
                for k in range(TOPK):
                    link(nc.vector.tensor_tensor(prod[:], hot[:, k], posn[:].rearrange("p e b -> p b e"), ALU.mult))
                    link(nc.vector.tensor_reduce(dest_f[:, k, :], prod[:], AX_X, ALU.add))
                link(nc.vector.tensor_scalar(dest_i[:, g], dest_f[:], float(g * GT * P), None, ALU.add))
                link(nc.vector.tensor_tensor(
                    tcmp[:], tiles_inc[:].rearrange("p (o e) -> p o e", o=1).to_broadcast([P, GT, E]),
                    wide(con[:, C_TILE:C_TILE + GT], [P, GT, E], "p (i o) -> p i o"), ALU.is_le))
                link(nc.vector.tensor_reduce(texp[:], tcmp[:], AX_X, ALU.add))
                link(nc.vector.tensor_scalar(tile_expert[:, GT * g:GT * g + GT], texp[:], float(E - 1), None, ALU.min))
                dve.wait_ge(gexp_ready, g + 1)
                link(nc.vector.tensor_scalar(gden[:], gexp[:], 1.0, None, ALU.add))
                weight = rows[:, GB * g:GB * g + GB, :, D + 1]
                link(nc.vector.reciprocal(weight[:, :, 0], gden[:]))
                nc.vector.tensor_tensor(weight[:, :, 1], gexp[:], weight[:, :, 0], ALU.mult).then_inc(routed, 1)

            def after(n):
                if n == ROUTE:
                    choose(0, 0)
                if n == ROUTE + 1:
                    choose(0, 1)
                    count(0)
                if n == ROUTE + 2:
                    read_counts(0, bank[BK_XT])
                if n == ROUTE + 3:
                    route_rows(0)

            dve.wait_ge(ld_x[0], 16)
            for n in range(-4, 0):
                step(n, n % U)
            for i in range(1, 4):
                dve.wait_ge(ld_x[i], 16)
            for n in range(0, U):
                step(n, n % U)
            loop_steps(dve, step, U, ROUTE)
            for n in range(ROUTE, ROUTE + U):
                step(n, n % U)
                after(n)
            loop_steps(dve, step, ROUTE + U, B - U)
            for n in range(B - U, B + 3):
                step(n, n % U)
            for k in range(TOPK):
                choose(1, k)
            count(1)

            def tile_hidT(i, p):
                need(dve, pe_A, i + 1)
                need(dve, pe_Y, i - 1)
                nc.vector.tensor_copy(hidT[:, p], bank[BK_KQ][:, 0:2 * P].rearrange("p (c t) -> p c t", c=2)).then_inc(
                    dve_hidT, 1)

            def tile_y(i, r, q):
                need(dve, pe_Y, i + 1)
                need(dve, y_sent[r], 16 * q)
                nc.vector.tensor_scalar(ys[:, r, :], bank[BK_PV][:, 0:D], xs[:, r, D + 1:D + 2], None,
                                        ALU.mult).then_inc(dve_y, 1)

            def tile_hid(i, p):
                need(dve, act_silu, i + 1)
                need(dve, pe_A, i - 1)
                nc.vector.tensor_tensor(hid[:, p, :], bank[BK_MAX + p][:, 0:H], silu[:, p, :], ALU.mult).then_inc(
                    dve_hid, 1)

            def tile_step(i, r, q, qy):
                if not isinstance(i, int) or i >= 2:
                    tile_hidT(i - 2, r % 2)
                    tile_y(i - 2, (r - 2) % R, qy)
                if not isinstance(i, int) or i < TILES:
                    tile_hid(i, r % 2)

            def combine(b, r, q):
                dve.wait_ge(ld_yb[r], 16 * (q + 1))
                nc.vector.tensor_tensor(batch(b), batch(b), yb[:, r, 0, :], ALU.add).then_inc(dve_y0, 1)
                dve.wait_ge(dve_y0, b + 1)
                nc.vector.tensor_tensor(batch(b), batch(b), yb[:, r, 1, :], ALU.add).then_inc(dve_out, 1)

            for i in range(R):
                tile_step(i, i, 0, 0)
                if i == 1:
                    read_counts(1, bank[BK_TAIL])
                if i == 2:
                    route_rows(1)
            with dve.Fori(1, COMBINE) as q:
                for r in range(R):
                    tile_step(q * R + r, r, q, q - 1 if r < 2 else q)
            for i in range(COMBINE * R, TILES + 2):
                tile_step(i, i % R, i // R, (i - 2) // R)
                b = i - COMBINE * R - 2
                if 0 <= b < GB:
                    combine(b, b % R, b // R)
            for b in range(GB, B):
                combine(b, b % R, b // R)

        @block.tensor
        def _(pe):
            ident = con[:, C_IDENT:C_IDENT + P]
            pe.wait_ge(ld_con, 16)
            pe.wait_ge(ld_w, 16)
            pe.wait_ge(bias_rows, 48)
            pe.wait_ge(sg, 7)
            pe.wait_ge(su, 7)

            def mm(o, lhsT, rhs, start=True, stop=True):
                return nc.tensor.matmul(o, lhsT, rhs, start=start, stop=stop)

            def step(n, u):
                if live(n):
                    scores(n, u, 0)
                if live(n - 1):
                    weighted(n - 1, (u - 1) % 2, 1)
                if live(n + 2):
                    need(pe, dve_xn, n + 3)
                    need(pe, act_xnT, n + 2)
                    if isinstance(n, int) and n == ROUTE + 3:
                        pe.wait_ge(counts_read, 1)
                    nc.tensor.transpose(bank[BK_XT][:, 0:T], xn[:, u % 2, :], ident).then_inc(pe_a, 1)
                if live(n - 2):
                    need(pe, dve_x2n, n - 1)
                    need(pe, dve_mT, upto(n + 1))
                    nc.tensor.transpose(bank[BK_TAIL][:, 0:T], x2n[:, u % 2, :], ident).then_inc(pe_j, 1)
                if live(n):
                    scores(n, u, 1)
                if live(n - 2):
                    need(pe, act_x2T, n - 1)
                    mm(bank[BK_TAIL][:, 0:E], x2T[:, u % 2, :], wat[:, WG:WG + E]).then_inc(pe_k, 1)
                if live(n + 1):
                    p = (u + 1) % 2
                    need(pe, act_kq, n + 2)
                    need(pe, dve_max, n + 1)
                    for half, done in enumerate((pe_d0, pe_d1)):
                        dst = bank[BK_MAX + half]
                        mm(dst[:].rearrange("p (h s) -> p h s", h=HALF), row0_b[:],
                           maskb[:, bass.ds((n + 1) * T, T)].rearrange("p (o s) -> p o s", o=1).to_broadcast(
                               [P, HALF, T]), stop=False)
                        for j in range(HALF):
                            last = mm(dst[:, j * T:j * T + T], q4b[:, p, j, :], kb[:, p, half, :], start=False,
                                      stop=j == HALF - 1)
                        last.then_inc(done, 1)
                if live(n - 1):
                    need(pe, dve_upd, n)
                    need(pe, dve_logit, n - 1)
                    nc.tensor.transpose(bank[BK_TAIL][:, 0:T], upd[:, (u - 1) % 2, :], ident).then_inc(pe_h, 1)
                if live(n + 1):
                    r = (u + 1) % 4
                    need(pe, dve_upd, n)
                    if isinstance(n, int) and n == 0:
                        pe.wait_ge(act_v, 1)
                    need(pe, ld_ctx[r], ctx_loads(n, u, 1))
                    dst = bank[BK_PV][:, 0:D]
                    for c in range(2):
                        mm(dst, ctx[:, r, c, :], wat[:, WV + D * c:WV + D * c + D], start=c == 0, stop=False)
                    mm(dst, ones_b[:], bias3[:, BV:BV + D], start=False).then_inc(pe_c, 1)
                if live(n - 1):
                    dst = bank[BK_TAIL][:, 0:D]
                    need(pe, act_updT, n)
                    mm(dst, updT[:, (u - 1) % 2, :], wat[:, WO + D:WO + 2 * D], stop=False)
                    mm(dst, xnT[:, (u - 1) % 4, :], wat[:, WO:WO + D], start=False, stop=False)
                    mm(dst, ones_b[:], bias3[:, BO:BO + D], start=False).then_inc(pe_i, 1)
                if live(n + 2):
                    r = (u + 2) % 4
                    need(pe, ld_ctx[r], ctx_loads(n, u, 2))
                    need(pe, act_xnT, n + 3)
                    need(pe, dve_q, n + 2)
                    for c in range(2):
                        mm(bank[BK_KQ][:, 0:T], wat[:, WK + D * c:WK + D * c + D], ctx[:, r, c, :], start=c == 0,
                           stop=c == 1)
                    mm(bank[BK_KQ][:, T:2 * T], wat[:, WQ:WQ + D], xnT[:, r, :]).then_inc(pe_b, 1)
                if live(n + 1):
                    need(pe, dve_mneg, n + 2)
                    need(pe, dve_x1, n)
                    nc.tensor.transpose(bank[BK_TAIL][:].bitcast(BF16)[:, 0:T], mneg[:, (u + 1) % 2, :],
                                        ident_b[:]).then_inc(pe_e, 1)
                if live(n):
                    need(pe, act_v, upto(n + 2))
                    weighted(n, u % 2, 0)

            def ctx_loads(n, u, ahead):
                if isinstance(n, int):
                    return 16 * ((n + ahead) // 4 + 1)
                return (n - u) * 4 + 16 * ((u + ahead) // 4 + 1)

            def weighted(n, p, half):
                need(pe, (act_exp0, act_exp1)[half], n + 1)
                for h in range(HALF * half, HALF * half + HALF):
                    last = mm(bank[BK_PV][:, h * (HD + 1):(h + 1) * (HD + 1)], attn[:, p, h, :], vaug[:, p, h, :])
                if half == 1:
                    last.then_inc(pe_g, 1)

            def scores(n, u, half):
                p = u % 2
                dst = bank[BK_SC + half]
                if half == 0:
                    need(pe, dve_mT, n + 1)
                need(pe, (act_exp0, act_exp1)[half], n)
                mm(dst[:].rearrange("p (h t) -> p h t", h=HALF), kz[:, p, half, :], q4[:, p], stop=False)
                for j in range(HALF):
                    last = mm(dst[:, j * T:j * T + T], sel_b[:, HALF * half + j, :], mT[:, p, :], start=False, stop=j == HALF - 1)
                last.then_inc((pe_f0, pe_f1)[half], 1)

            def count(g, dst):
                pe.wait_ge(counts_in, g + 1)
                mm(dst[:, 0:E], tri_b[:], rowsum_b[:])
                mm(dst[:, E:2 * E], ones_b[:], rowsum_b[:]).then_inc(counted, 1)

            def after(n):
                if n == ROUTE + 2:
                    pe.wait_ge(act_xnT, n + 3)
                    count(0, bank[BK_XT])

            run_attention(pe, step, after)

            def expert(i):
                return pe.value_load(tile_expert[0:1, bass.ds(i, 1)], min_val=0, max_val=E - 1)

            def tile_T(i, r, q):
                need(pe, ld_xs[r], (q + 1) * 16)
                need(pe, act_exT, i)
                nc.tensor.transpose(bank[BK_XT][:, 0:P], xs[:, r, 0:D], ident).then_inc(pe_T, 1)

            def tile_H(i, p, e):
                need(pe, act_exT, i + 1)
                need(pe, dve_hid, i - 1)
                dst = bank[BK_MAX + p][:]
                mm(dst, exT[:, p, :], w01s[:, bass.ds(e * (2 * H), 2 * H)], stop=False)
                mm(dst, ones_b[:], bias3[:, bass.ds(e * (2 * H) + B01, 2 * H)], start=False).then_inc(pe_H, 1)

            def tile_A(i, p):
                need(pe, dve_hid, i + 1)
                need(pe, dve_hidT, i)
                for c in range(2):
                    last = nc.tensor.transpose(bank[BK_KQ][:, c * P:c * P + P], hid[:, p, c * P:c * P + P], ident)
                last.then_inc(pe_A, 1)

            def tile_Y(i, p, e):
                need(pe, dve_hidT, i + 1)
                need(pe, dve_y, i)
                dst = bank[BK_PV][:, 0:D]
                for c in range(2):
                    mm(dst, hidT[:, p, c, :], w2s[:, bass.ds(e * (2 * D) + c * D, D)], start=c == 0, stop=False)
                mm(dst, ones_b[:], bias3[:, bass.ds(e * D + B2, D)], start=False).then_inc(pe_Y, 1)

            def tile_step(i, r, q, ahead=True):
                static = isinstance(i, int)
                if not static or i >= 2:
                    tile_A(i - 2, r % 2)
                if not static or i < TILES:
                    tile_H(i, r % 2, expert(i))
                if not static or i >= 2:
                    tile_Y(i - 2, r % 2, expert(i - 2))
                if not static or i + 2 < TILES:
                    tile_T(i + 2, (r + 2) % R, q if r < R - 2 else q + 1)

            pe.wait_ge(ld_ew, 32)
            tile_T(0, 0, 0)
            tile_T(1, 1, 0)
            for i in range(R):
                tile_step(i, i, 0)
                if i == 0:
                    count(1, bank[BK_TAIL])
            pe.wait_ge(routed, 2)
            with pe.Fori(1, TILES // R) as q:
                for r in range(R):
                    tile_step(q * R + r, r, q)
            for i in range(TILES // R * R, TILES + 2):
                tile_step(i, i % R, i // R)


def kernel(**inputs):
    import numpy as np
    import concourse.bacc as bacc
    from concourse.bass_utils import run_bass_kernel_spmd

    def get(name):
        return np.asarray(inputs[name])

    def c(a):
        return np.ascontiguousarray(a)

    x, context, mask = get("x"), get("ctx_2048"), get("mask_BxS2_fk1")
    w_src, w_tgt, w_out = get("L0_xattn_W_src"), get("L0_xattn_W_tgt"), get("L0_xattn_W_out")
    b_src = get("L0_xattn_b_src")
    ctxT = c(context.transpose(0, 2, 1).reshape(B, 2, P, T).transpose(0, 2, 1, 3))
    wkT, wvT = w_src[:D].T.reshape(2, P, D), w_src[D:].T.reshape(2, P, D)
    woT = w_out.T.reshape(2, P, D)
    w_attn = c(np.concatenate([wkT[0], wkT[1], wvT[0], wvT[1], w_tgt.T, woT[0], woT[1], get("L0_ffn_gate_w").T], 1))
    cols = c(np.concatenate([b_src[:D, None], get("L0_xattn_b_tgt")[:, None], mask.T], 1))
    biases = c(np.concatenate([b_src[D:], get("L0_xattn_b_out"),
                               np.concatenate([get("L0_ffn_b0"), get("L0_ffn_b1")], 1).reshape(-1),
                               get("L0_ffn_b2").reshape(-1)]).reshape(P, BIASES // P))
    w01 = c(np.concatenate([get("L0_ffn_w0"), get("L0_ffn_w1")], 1).transpose(2, 0, 1).reshape(P, E * 2 * H))
    w2 = c(get("L0_ffn_w2").reshape(E, D, 2, P).transpose(3, 0, 2, 1).reshape(P, E * 2 * D))
    p = np.arange(P)
    consts = np.zeros((P, C_COLS), np.float32)
    consts[:, C_IDENT:C_IDENT + P] = np.eye(P)
    consts[:, C_TRI:C_TRI + P] = p[:, None] < p[None, :]
    consts[:, C_PATT:C_PATT + HALF] = (p % 64 // HD)[:, None] == np.arange(HALF)[None, :]
    consts[:, C_SEL:C_SEL + HEADS] = (p // 64 * HALF + p % HALF)[:, None] == np.arange(HEADS)[None, :]
    consts[:, C_ROW0] = p == 0
    consts[:, C_REV:C_REV + E] = E - np.arange(E)[None, :]
    consts[:, C_TILE:C_TILE + GT] = np.arange(GT)[None, :]
    token = (np.arange(B)[None, :, None] * T + p[:, None, None]) * TOPK + np.arange(TOPK)[None, None, :]
    arrays = {
        "x": c(x), "ctxT": ctxT, "w_attn": w_attn, "cols": cols, "mask_row": c(mask.reshape(1, -1)[0]),
        "gate_b": c(get("L0_ffn_gate_b")), "biases": biases, "w01": w01, "w2": w2, "consts": consts,
        "ids": c(token.reshape(P, B * TOPK).astype(np.int32)),
    }
    nc = bacc.Bacc("TRN2", target_bir_lowering=False, num_devices=1)
    handles = {k: nc.dram_tensor(k, v.shape, mybir.dt.from_np(v.dtype), kind="ExternalInput").ap()
               for k, v in arrays.items()}
    out = nc.dram_tensor("out", (B, T, D), F32, kind="ExternalOutput").ap()
    build(nc, *handles.values(), out)
    r = run_bass_kernel_spmd(nc, [arrays], core_ids=[0])
    return r.results[0]["out"]
```

```python
from contextlib import ExitStack

import concourse.bass as bass
from concourse import mybir

F32 = mybir.dt.float32
BF16 = mybir.dt.bfloat16
I32 = mybir.dt.int32
ALU = mybir.AluOpType
ACT = mybir.ActivationFunctionType
AX_X = mybir.AxisListType.X

P = 128
B, T, D, DS = 32, 128, 128, 256
HEADS, HD = 8, 16
HALF = HEADS // 2
E, H, TOPK = 8, 256, 2
EPS = 1e-5
FAR = -1.0e30
GROUPS = ((0, 19), (19, 13))
GB = max(size for _, size in GROUPS)
GTILES = [size * T * TOPK // P + E - 1 for _, size in GROUPS]
GT = max(GTILES)
TILES = sum(GTILES)
RC = D + 2
NOWHERE = 1 << 20
U = 4
R = 8
ROUTE = 20
SEND = ROUTE + 6
COMBINE = 7
AHEAD = 8
TURNS_SENT = -(-2 * (TOPK * GROUPS[1][1] - AHEAD) // R)
assert GTILES[0] < (COMBINE - 1) * R and COMBINE * R + 2 + GROUPS[0][1] <= TILES
assert ROUTE % U == 0 and ROUTE - 2 >= GROUPS[0][1] - 1 and ROUTE + 7 < B

PAIRS = [(lo, min(lo + 2, GROUPS[0][1])) for lo in range(0, GROUPS[0][1], 2)]
SUMS = 4
LAST = [(lo, min(lo + 4, B)) for lo in range(GROUPS[1][0], B, 4)]
X_PIECES = (0, 2, 8, 16, B)
MASK_PIECES = (0, U, 3 * U, B)
WK, WV, WQ, WO, WG = 0, 2 * D, 4 * D, 5 * D, 7 * D
W_COLS = 7 * D + E
X0, XB0, X2 = 0, H, H + H // P
XB2 = X2 + 2 * D
X1 = XB2 + D // 2
XB1, X_COLS = X1 + H, X1 + H + H // P
C_IDENT, C_TRI, C_PATT, C_SEL = 0, P, 2 * P, 2 * P + HALF
C_REV, C_TILE = C_SEL + HEADS, C_SEL + HEADS + E
C_COLS = C_TILE + GT
BV, BO = 0, D
BIASES = 2 + E


def need(engine, sem, count):
    if not isinstance(count, int) or count > 0:
        engine.wait_ge(sem, count)


def live(b):
    return not isinstance(b, int) or 0 <= b < B


def stand(engine, waits_over):
    engine.sem_inc(waits_over, 1)


def upto(count):
    return min(count, B) if isinstance(count, int) else count


def build(nc, x, ctxT, w_attn, cols, mask, mask_row, gate_b, biases, w02, w1, consts, ids, out):
    with ExitStack() as stack:
        def sb(name, shape, dt=F32):
            return stack.enter_context(nc.sbuf_tensor(name, shape, dt))

        def sem(name):
            return stack.enter_context(nc.semaphore(name))

        xres = sb("xres", [P, B, D])
        rows = sb("rows", [P, B, TOPK, RC])
        ctx = sb("ctx", [P, 4, 2, T])
        wat = sb("wat", [P, W_COLS])
        ew = sb("ew", [P, E * X_COLS])
        bias3 = sb("bias3", [P, 2 * D], BF16)
        bias_f = sb("bias_f", [BIASES, D])
        bias_r = sb("bias_r", [BIASES, 2, D])
        bias_p = sb("bias_p", [BIASES, 3, D], BF16)
        colsb = sb("colsb", [P, 2 + B])
        maskr = sb("maskr", [P, B * T])
        maskn = sb("maskn", [B, T])
        maskb = sb("maskb", [B, T], BF16)
        keyb = sb("keyb", [P, B])
        gbias = sb("gbias", [P, E])
        con = sb("con", [P, C_COLS])
        idsb = sb("idsb", [P, B * TOPK], I32)
        ident_b = sb("ident_b", [P, P], BF16)
        tri_b = sb("tri_b", [P, P], BF16)
        ones_b = sb("ones_b", [P, P], BF16)
        sel_b = sb("sel_b", [P, HEADS, P], BF16)
        onesf = sb("onesf", [P, E * GB])
        mhalf = sb("mhalf", [P, 1])
        warm = sb("warm", [P, 1])
        blank = sb("blank", [P, RC])

        st1 = sb("st1", [P, 2, 6])
        mv1 = sb("mv1", [P, 4, 2])
        ve1 = sb("ve1", [P, 4])
        rs1 = sb("rs1", [P, 4])
        st2 = sb("st2", [P, 2, 6])
        mv2 = sb("mv2", [P, 4, 2])
        ve2 = sb("ve2", [P, 4])
        rs2 = sb("rs2", [P, 4])
        xn = sb("xn", [P, 2, D])
        xnT = sb("xnT", [P, 4, T])
        kz = sb("kz", [P, 2, 2, T])
        headmask = sb("headmask", [P, 2, HALF, T])
        kb = sb("kb", [P, 2, B, T], BF16)
        q4 = sb("q4", [P, 2, HALF, T])
        q4b = sb("q4b", [P, 2, 2, HALF, T], BF16)
        nmax = sb("nmax", [P, 2, HEADS])
        mneg = sb("mneg", [P, 2, P], BF16)
        mT = sb("mT", [P, 2, T], BF16)
        attn = sb("attn", [P, 2, HEADS, T])
        vaug = sb("vaug", [P, 2, HEADS, HD + 1])
        rsum = sb("rsum", [P, 2, HEADS])
        upd = sb("upd", [P, 2, D])
        updT = sb("updT", [P, 2, T])
        x2n = sb("x2n", [P, 2, D])
        x2T = sb("x2T", [P, 2, T])
        logits = sb("logits", [P, B, E])

        top = sb("top", [P, 2, GB])
        first = sb("first", [P, 2, GB])
        eqs = sb("eqs", [P, GB, E])
        hot = sb("hot", [P, 2, GB, E])
        lower = sb("lower", [P, GB, E])
        gap = sb("gap", [P, GB])
        gexp = sb("gexp", [P, GB])
        gden = sb("gden", [P, GB])
        picked = sb("picked", [P, E * GB])
        running = sb("running", [P, E * GB])
        rowsum = sb("rowsum", [P, E])
        rowsum_b = sb("rowsum_b", [P, E], BF16)
        rowinc = sb("rowinc", [P, E])
        counts = sb("counts", [P, 2 * E])
        place = sb("place", [P, E])
        cnt_i = sb("cnt_i", [P, E], I32)
        tiles_f = sb("tiles_f", [P, E])
        tiles_inc = sb("tiles_inc", [P, E])
        posn = sb("posn", [P, E * GB])
        prod = sb("prod", [P, TOPK, GB, E])
        dest_f = sb("dest_f", [P, 2, GB])
        dest_i = sb("dest_i", [P, 2, B], I32)
        tcmp = sb("tcmp", [P, GT, E])
        texp = sb("texp", [P, GT])
        tile_column = sb("tile_column", [P, TILES], I32)

        xs = sb("xs", [P, R, RC])
        exT = sb("exT", [P, 2, P])
        wbuf = sb("wbuf", [P, 4, X_COLS])
        silu = sb("silu", [P, 2, 2, P])
        hidT = sb("hidT", [P, 2, 2, P])
        ys = sb("ys", [P, R, D])
        yb = sb("yb", [P, SUMS, 2, TOPK * D])

        sorted_rows = nc.dram_tensor("sorted_rows", (TILES * P, RC), F32, kind="Internal").ap()
        expert_out = nc.dram_tensor("expert_out", (B * T * TOPK, D), F32, kind="Internal").ap()

        bank = [stack.enter_context(nc.psum_tensor(f"bank{i}", [P, 512], F32)) for i in range(8)]
        BK_XT, BK_KQ, BK_MAX, BK_SC, BK_PV, BK_TAIL = 0, 1, 2, 4, 6, 7

        ld_x = [sem(f"ld_x{i}") for i in range(4)]
        ld_w = sem("ld_w")
        ld_con = sem("ld_con")
        ld_cols, ld_small = sem("ld_cols"), sem("ld_small")
        ld_bias = sem("ld_bias")
        ld_mask = [sem(f"ld_mask{i}") for i in range(3)]
        ld_ew = sem("ld_ew")
        ld_ctx = [sem(f"ld_ctx{i}") for i in range(4)]
        blanked = sem("blanked")
        filled_later = sem("filled_later")
        bias_rows, bias_rows_e = sem("bias_rows"), sem("bias_rows_experts")
        waits_over = sem("waits_over")
        filled, filled_half = sem("gpsimd_filled"), sem("vector_filled")
        bias_split, masked = sem("bias_split"), sem("mask_bf16")
        keyb_ready, idents_ready = sem("keyb_ready"), sem("bf16_constants")
        mask_rows = sem("mask_rows")
        pe_a, pe_b, pe_c, pe_d0, pe_d1, pe_e = (sem(f"pe_{k}") for k in (
            "xn_transposed", "kq", "v", "max0", "max1", "shift_transposed"))
        pe_f0, pe_f1, pe_g, pe_h, pe_i, pe_j, pe_k = (sem(f"pe_{k}") for k in (
            "scores0", "scores1", "weighted", "upd_transposed", "proj", "x2_transposed", "logits"))
        act_exp0, act_exp1, act_xnT, act_x2T, act_updT, act_v = (sem(f"act_{k}") for k in (
            "exp0", "exp1", "xnT", "x2T", "updT", "v"))
        dve_bn1, dve_agg1, dve_xn, dve_max, dve_mh, dve_mneg, dve_mT = (sem(f"dve_{k}") for k in (
            "bn1", "agg1", "xn", "max", "shift_high", "shift", "mT"))
        dve_k, dve_q, dve_rs, dve_upd, dve_x1, dve_bn2, dve_agg2, dve_x2n, dve_logit = (
            sem(f"dve_{k}") for k in ("k", "q", "rsum", "upd", "x1", "bn2", "agg2", "x2n", "logit"))
        pool_v1, pool_rs1, pool_v2, pool_rs2, pool_hm = (sem(f"pool_{k}") for k in (
            "var1", "rstd1", "var2", "rstd2", "headmask"))
        dve_qb = sem("dve_q_bf16")
        act_kq, act_rows = sem("act_kq_bf16"), sem("act_rows")
        route = sem("route_step")
        gap_ready, gexp_ready = sem("gap_ready"), sem("gexp_ready")
        counts_in, counted, counts_read, routed = (sem(k) for k in ("counts_in", "counted", "counts_read", "routed"))
        sent = [sem(f"rows_sent{g}") for g in range(len(GROUPS))]
        ld_xs = [sem(f"ld_tile{i}") for i in range(R)]
        y_sent = [sem(f"y_sent{i}") for i in range(R)]
        pe_T, pe_H1, pe_H0, pe_Y = (sem(f"pe_{k}") for k in ("tile_transposed", "hidden1", "hidden0", "y"))
        act_exT, act_silu, act_y = (sem(f"act_{k}") for k in ("exT", "silu", "y"))
        dve_hid, dve_w = sem("dve_hid"), sem("dve_w")
        ld_last = [sem(f"ld_last{i}") for i in range(len(LAST))]
        ld_yb = [sem(f"ld_yb{i}") for i in range(SUMS)]
        dve_y0, dve_out, st_out, dve_last = sem("dve_y0"), sem("dve_out"), sem("st_out"), sem("dve_last")

        block = stack.enter_context(nc.Block())
        experts = ew[:].rearrange("p (e c) -> p e c", e=E)

        def landing(lo, hi):
            at = GROUPS[1][0] * TOPK * RC
            flat = rows[:].rearrange("p b k c -> p (b k c)")[:, at:at + GROUPS[1][1] * TOPK * D]
            return flat.rearrange("p (b c) -> p b c", c=TOPK * D)[:, lo - GROUPS[1][0]:hi - GROUPS[1][0], :]

        def expert(engine, i):
            return engine.value_load(tile_column[0:1, bass.ds(i, 1)], min_val=0, max_val=(E - 1) * X_COLS)

        def loop_steps(engine, step, lo, hi):
            with engine.Fori(lo // U, hi // U) as q:
                base = engine.snap(q * U)
                for u in range(U):
                    step(base + u, u)

        def run_attention(engine, step, after=None):
            for n in range(-4, U):
                step(n, n % U)
                if after:
                    after(n)
            loop_steps(engine, step, U, ROUTE)
            for n in range(ROUTE, B + 3):
                step(n, n % U)
                if after:
                    after(n)

        @block.sync
        def _(sp):
            def load_x(i):
                lo, hi = X_PIECES[i:i + 2]
                sp.dma_start(xres[:, lo:hi, :], x[lo:hi].rearrange("b t d -> t b d")).then_inc(ld_x[i], 16)

            def load_mask(i):
                lo, hi = (b * T for b in MASK_PIECES[i:i + 2])
                sp.dma_start(maskr[:, lo:hi], mask_row[lo:hi].partition_broadcast(P)).then_inc(ld_mask[i], 16)

            load_x(0)
            sp.dma_start(wat[:], w_attn).then_inc(ld_w, 16)

            def step(n, u):
                b = n + 4
                if live(b):
                    need(sp, pe_c, b - 3)
                    sp.dma_start(ctx[:, u], ctxT[bass.ds(b, 1)].rearrange("b p c s -> p (b c) s")).then_inc(
                        ld_ctx[u], 16)

            for n in range(-4, 0):
                step(n, n % U)
                if n == -4:
                    sp.dma_start(bias_f[:], biases).then_inc(ld_bias, 16)
                    sp.dma_start(maskn[:], mask).then_inc(ld_bias, 16)
                    load_x(1)
            sp.wait_ge(masked, 1)
            sp.wait_ge(filled, 8)
            sp.wait_ge(filled_half, 1)
            for half in range(2):
                row = 64 - 64 * half
                sp.dma_start(kb[row:row + 1, half], maskb[:]).then_inc(mask_rows, 16)
            sp.wait_ge(bias_split, 5)
            for k in range(3):
                sp.dma_start(bias3[k:k + 1, :], bias_p[0:2, k, :]).then_inc(bias_rows, 16)
            load_mask(1)
            load_x(2)
            sp.dma_start(gbias[:], gate_b.partition_broadcast(P)).then_inc(ld_small, 16)
            sp.dma_start(idsb[:], ids).then_inc(ld_small, 16)
            load_mask(2)
            load_x(3)
            for n in range(0, 4):
                step(n, n % U)
            sp.wait_ge(filled_later, 4)
            for k in range(3):
                sp.dma_start(experts[k:k + 1, :, XB2:X1].bitcast(BF16), bias_p[2:BIASES, k, :]).then_inc(
                    bias_rows_e, 16)
            sp.dma_start(experts[:, :, X0:XB2], w02).then_inc(ld_ew, 16)
            sp.dma_start(experts[:, :, X1:X_COLS], w1).then_inc(ld_ew, 16)
            loop_steps(sp, step, 4, B - 4)

            def load_tile(i, r, q):
                need(sp, y_sent[r], 16 * q)
                sp.dma_start(xs[:, r, :], sorted_rows[bass.ds(i * P, P), :]).then_inc(ld_xs[r], 16)

            pairs = expert_out.rearrange("(b t k) d -> b t (k d)", b=B, k=TOPK)

            def load_pair(m):
                need(sp, dve_out, m - SUMS + 1)
                lo, hi = PAIRS[m]
                sp.dma_start(yb[:, m % SUMS, 0:hi - lo, :], pairs[lo:hi].rearrange("b t c -> t b c")).then_inc(
                    ld_yb[m % SUMS], 16)

            def load_tiles(lo, hi, combining=False):
                i = lo
                while i < hi:
                    if i % R or i + R > hi or combining:
                        load_tile(i, i % R, i // R)
                        if combining and i % 2 == 0 and (i - COMBINE * R) // 2 < len(PAIRS):
                            load_pair((i - COMBINE * R) // 2)
                        i += 1
                    else:
                        with sp.Fori(i // R, hi // R) as q:
                            for r in range(R):
                                load_tile(q * R + r, r, q)
                        i = hi // R * R

            sp.wait_ge(sent[0], 16 * TOPK * GROUPS[0][1])
            sp.wait_ge(blanked, 16)
            for i in range(R):
                load_tile(i, i, 0)
            load_tiles(R, GTILES[0])
            sp.wait_ge(sent[1], 16 * TOPK * GROUPS[1][1])
            load_tiles(GTILES[0], COMBINE * R)
            for r in range(R):
                sp.wait_ge(y_sent[r], 16 * len(range(r, GTILES[0], R)))
            load_tiles(COMBINE * R, TILES, combining=True)
            for r in range(R):
                sp.wait_ge(y_sent[r], 16 * len(range(r, TILES, R)))
            for i, (lo, hi) in enumerate(LAST):
                sp.dma_start(landing(lo, hi), pairs[lo:hi].rearrange("b t c -> t b c")).then_inc(ld_last[i], 16)

        @block.scalar
        def _(act):
            def load_mask(i):
                lo, hi = (b * T for b in MASK_PIECES[i:i + 2])
                act.dma_start(maskr[:, lo:hi], mask_row[lo:hi].partition_broadcast(P)).then_inc(ld_mask[i], 16)

            act.dma_start(con[:], consts).then_inc(ld_con, 16)
            act.dma_start(colsb[:], cols).then_inc(ld_cols, 16)
            act.dma_start(maskr[:, 0:MASK_PIECES[1] * T], mask_row[0:MASK_PIECES[1] * T].partition_broadcast(P)).then_inc(
                ld_mask[0], 16)
            act.wait_ge(filled, 1)
            nc.scalar.activation(warm[:], mhalf[:], ACT.Exp)

            def step(n, u):
                if live(n):
                    p = u % 2
                    for half, (scored, done) in enumerate(((pe_f0, act_exp0), (pe_f1, act_exp1))):
                        need(act, scored, n + 1)
                        need(act, pe_g, n - 1)
                        stand(act, waits_over)
                        nc.scalar.activation(
                            attn[:, p, HALF * half:HALF * half + HALF, :],
                            bank[BK_SC + half][:].rearrange("p (h t) -> p h t", h=HALF), ACT.Exp,
                            bias=keyb[:, bass.ds(n, 1)], scale=HD ** -0.5).then_inc(done, 1)
                        if half == 0:
                            transposed(n, u)
                else:
                    transposed(n, u)
                if live(n - 1):
                    p = (u - 1) % 2
                    need(act, pe_h, n)
                    need(act, pe_i, n - 2)
                    nc.scalar.copy(updT[:, p, :], bank[BK_TAIL][:, 0:T]).then_inc(act_updT, 1)
                if live(n + 1):
                    p = (u + 1) % 2
                    need(act, pe_c, n + 2)
                    need(act, pe_g, n)
                    stand(act, waits_over)
                    nc.scalar.activation(vaug[:, p, :, 0:HD],
                                         bank[BK_PV][:, 0:D].rearrange("p (h d) -> p h d", h=HEADS),
                                         ACT.Identity, scale=colsb[:, bass.ds(n + 3, 1)]).then_inc(act_v, 1)
                if live(n - 2):
                    p = u % 2
                    need(act, dve_x2n, n - 1)
                    src = x2n[:, p, :].rearrange("p (o d) -> p o d", o=1).to_broadcast([P, TOPK, D])
                    nc.scalar.copy(rows[:, bass.ds(n - 2, 1), :, 0:D].rearrange("p b k d -> p (b k) d"),
                                   src).then_inc(act_rows, 1)
                if live(n + 2):
                    p = u % 2
                    need(act, dve_k, n + 3)
                    stand(act, waits_over)
                    for half in range(2):
                        s = slice(64 * half, 64 * half + 64)
                        nc.scalar.copy(kb[s, half, bass.ds(n + 2, 1), :].rearrange("p b s -> p (b s)"),
                                       kz[s, p, half, :])
                    need(act, pe_d1, n + 1)
                    need(act, dve_q, n + 3)
                    nc.scalar.copy(q4b[64:128, 1, p], q4[64:128, p]).then_inc(act_kq, 1)

            def transposed(n, u):
                if live(n + 2):
                    r = (u + 2) % 4
                    need(act, pe_a, n + 3)
                    need(act, pe_i, n - 1)
                    nc.scalar.copy(xnT[:, r, :], bank[BK_XT][:, 0:T]).then_inc(act_xnT, 1)
                if live(n - 2):
                    p = u % 2
                    need(act, pe_j, n - 1)
                    need(act, pe_k, n - 3)
                    nc.scalar.copy(x2T[:, p, :], bank[BK_TAIL][:, 0:T]).then_inc(act_x2T, 1)

            def weigh(g):
                act.wait_ge(gap_ready, g + 1)
                size = GROUPS[g][1]
                nc.scalar.activation(gexp[:, 0:size], gap[:, 0:size], ACT.Exp).then_inc(gexp_ready, 1)

            def after(n):
                if n == -1:
                    act.wait_ge(keyb_ready, 1)
                if n == U - 1:
                    act.dma_start(sorted_rows.rearrange("(i p) c -> p i c", p=P),
                                  blank[:].rearrange("p (i c) -> p i c", i=1).to_broadcast([P, TILES, RC])).then_inc(
                                      blanked, 16)
                if n == ROUTE + 2:
                    weigh(0)

            run_attention(act, step, after)

            def tile_T(i, p):
                need(act, pe_T, i + 1)
                need(act, pe_H0, i - 1)
                nc.scalar.copy(exT[:, p, :], bank[(BK_XT, BK_TAIL)[p]][:, 0:P]).then_inc(act_exT, 1)

            def tile_silu(i, p, w):
                need(act, pe_H1, i + 1)
                need(act, dve_hid, i - 1)
                for c in range(2):
                    last = nc.scalar.activation(silu[:, p, c, :], bank[BK_MAX + p][:, c * P:c * P + P], ACT.Silu,
                                                bias=wbuf[:, w, XB1 + c:XB1 + c + 1])
                last.then_inc(act_silu, 1)

            def tile_y(i, r, q):
                need(act, pe_Y, i + 1)
                need(act, y_sent[r], 16 * q)
                nc.scalar.activation(ys[:, r, :], bank[(BK_KQ, BK_PV)[r % 2]][:, 0:D], ACT.Identity,
                                     scale=xs[:, r, D + 1:D + 2]).then_inc(act_y, 1)

            def tile_step(i, r, q, qy):
                static = isinstance(i, int)
                if not static or i < TILES:
                    tile_silu(i, r % 2, r % 4)
                if not static or i >= 1:
                    tile_y(i - 1, (r - 1) % R, qy)
                if not static or i + 2 < TILES:
                    tile_T(i + 2, r % 2)

            def store(lo, hi):
                act.dma_start(out[lo:hi].rearrange("b t d -> t b d"), xres[:, lo:hi, :]).then_inc(st_out, 16)

            weigh(1)
            nc.scalar.activation(warm[:], mhalf[:], ACT.Silu)
            for i in range(2):
                tile_T(i, i)
            for i in range(R):
                tile_step(i, i, 0, 0)
            with act.Fori(1, COMBINE) as q:
                for r in range(R):
                    tile_step(q * R + r, r, q, q - 1 if r < 1 else q)
            for i in range(COMBINE * R, TILES + 1):
                tile_step(i, i % R, i // R, (i - 1) // R)
                m = (i - COMBINE * R) // 2 - 2
                if i % 2 and 0 <= m < len(PAIRS):
                    act.wait_ge(dve_out, m + 1)
                    store(*PAIRS[m])
            for m in range((TILES - COMBINE * R) // 2 - 2, len(PAIRS)):
                act.wait_ge(dve_out, m + 1)
                store(*PAIRS[m])
            for i, piece in enumerate(LAST):
                act.wait_ge(dve_last, i + 1)
                store(*piece)
            act.wait_ge(st_out, 16 * (len(PAIRS) + len(LAST)))

        @block.gpsimd
        def _(pool):
            fills = ((mhalf[:], -0.5), (q4b[:].bitcast(F32), 0.0), (kb[:, 1].bitcast(F32), 0.0), (kz[:], 0.0),
                     (bias3[:].bitcast(F32), 0.0), (ones_b[:], 1.0), (mneg[:].bitcast(F32), 0.0), (vaug[:], 1.0))
            for dst, value in fills:
                nc.gpsimd.memset(dst, value).then_inc(filled, 1)

            def after(n):
                if n == -4:
                    pool.wait_ge(ld_con, 16)
                    pool.wait_ge(ld_mask[0], 16)
                if n == 0:
                    pool.wait_ge(ld_mask[1], 16)
                if n == U - 1:
                    pool.wait_ge(ld_mask[2], 16)

            def rstd(done, v, agg, mv, ve, rs, c, r):
                need(pool, agg, c)
                stand(pool, waits_over)
                nc.gpsimd.tensor_scalar(ve[:, r:r + 1], mv[:, r, 1:2], EPS, None, ALU.add).then_inc(v, 1)
                need(pool, v, c)
                nc.gpsimd.tensor_tensor(rs[:, r:r + 1], ve[:, r:r + 1], mhalf[:], ALU.pow).then_inc(done, 1)

            patt = con[:, C_PATT:C_PATT + HALF].rearrange("p (j o) -> p j o", o=1).to_broadcast([P, HALF, T])

            def step(n, u):
                if live(n + 4):
                    need(pool, dve_xn, n + 1)
                    rstd(pool_rs1, pool_v1, dve_agg1, mv1, ve1, rs1, n + 5, u)
                if live(n + 3):
                    need(pool, dve_q, n + 2)
                    stand(pool, waits_over)
                    mrow = maskr[:, bass.ds((n + 3) * T, T)].rearrange("p (o t) -> p o t", o=1)
                    nc.gpsimd.tensor_tensor(headmask[:, (u + 1) % 2], mrow.to_broadcast([P, HALF, T]), patt,
                                            ALU.mult).then_inc(pool_hm, 1)
                if live(n - 1):
                    need(pool, dve_x2n, n - 4)
                    rstd(pool_rs2, pool_v2, dve_agg2, mv2, ve2, rs2, n, (u - 1) % 4)

            def send(g, b, k):
                nc.gpsimd.indirect_dma_start(
                    out=sorted_rows,
                    out_offset=bass.IndirectOffsetOnAxis(ap=dest_i[:, k, b:b + 1], axis=0),
                    in_=rows[:, b, k, :], in_offset=None,
                    bounds_check=TILES * P - 1, oob_is_err=False).then_inc(sent[g], 16)

            for n in range(-4, U):
                step(n, n % U)
                after(n)
                if n == -4:
                    nc.gpsimd.memset(experts[:, :, XB2:X1], 0.0).then_inc(filled_later, 1)
                    nc.gpsimd.memset(onesf[:], 1.0).then_inc(filled_later, 1)
                    nc.gpsimd.memset(blank[:], 0.0).then_inc(filled_later, 1)
                    pool.wait_ge(filled_later, 3)
                    nc.gpsimd.memset(blank[:, D:D + 1].bitcast(I32), NOWHERE).then_inc(filled_later, 1)
            loop_steps(pool, step, U, ROUTE)
            for n in range(ROUTE, SEND):
                step(n, n % U)
            waiting = [(b, k) for b in range(GROUPS[0][1]) for k in range(TOPK)]
            def send_some(count):
                for b, k in waiting[:count]:
                    send(0, b, k)
                del waiting[:count]

            pool.wait_ge(blanked, 16)
            pool.wait_ge(routed, 1)
            pool.wait_ge(act_rows, GROUPS[0][1])
            for n in range(SEND, B + 3):
                send_some(2 if live(n + 3) else 2)
                step(n, n % U)
                send_some(3 if live(n + 3) else 3)
            send_some(len(waiting))

            def send_y(i, r):
                need(pool, act_y, i + 1)
                stand(pool, waits_over)
                nc.gpsimd.indirect_dma_start(
                    out=expert_out,
                    out_offset=bass.IndirectOffsetOnAxis(ap=xs[:, r, D:D + 1].bitcast(I32), axis=0),
                    in_=ys[:, r, :], in_offset=None,
                    bounds_check=B * T * TOPK - 1, oob_is_err=False).then_inc(y_sent[r], 16)

            waiting = [(b, k) for b in range(GROUPS[1][0], B) for k in range(TOPK)]
            pool.wait_ge(act_rows, B)
            pool.wait_ge(routed, 2)
            for b, k in waiting[:AHEAD]:
                send(1, b, k)
            for i in range(TURNS_SENT * R):
                send_y(i, i % R)
                if i % 2 == 0:
                    for b, k in waiting[AHEAD + i // 2:AHEAD + i // 2 + 1]:
                        send(1, b, k)
            with pool.Fori(TURNS_SENT, TILES // R) as q:
                base = pool.snap(q * R)
                for r in range(R):
                    send_y(base + r, r)
            for i in range(TILES // R * R, TILES):
                send_y(i, i % R)

        @block.vector
        def _(dve):
            nc.vector.memset(kb[:, 0].bitcast(F32), 0.0).then_inc(filled_half, 1)

            def prepare():
                dve.wait_ge(ld_bias, 32)
                nc.vector.tensor_scalar(maskb[:], maskn[:], 0.0, FAR, ALU.is_equal, ALU.mult).then_inc(masked, 1)
                nc.vector.tensor_copy(bias_p[:, 0, :], bias_f[:]).then_inc(bias_split, 1)
                dve.wait_ge(bias_split, 1)
                nc.vector.tensor_tensor(bias_r[:, 0, :], bias_f[:], bias_p[:, 0, :], ALU.subtract).then_inc(bias_split, 1)
                dve.wait_ge(bias_split, 2)
                nc.vector.tensor_copy(bias_p[:, 1, :], bias_r[:, 0, :]).then_inc(bias_split, 1)
                dve.wait_ge(bias_split, 3)
                nc.vector.tensor_tensor(bias_r[:, 1, :], bias_r[:, 0, :], bias_p[:, 1, :], ALU.subtract).then_inc(
                    bias_split, 1)
                dve.wait_ge(bias_split, 4)
                nc.vector.tensor_copy(bias_p[:, 2, :], bias_r[:, 1, :]).then_inc(bias_split, 1)
                dve.wait_ge(ld_cols, 16)
                nc.vector.tensor_scalar(keyb[:], colsb[:, 2:2 + B], 0.0, FAR, ALU.is_equal, ALU.mult).then_inc(
                    keyb_ready, 1)
                dve.wait_ge(ld_con, 16)
                nc.vector.tensor_copy(ident_b[:], con[:, C_IDENT:C_IDENT + P]).then_inc(idents_ready, 1)

            def batch(b):
                return xres[:, bass.ds(b, 1), :].rearrange("p b d -> p (b d)")

            def stats(b, v, bn, st):
                stand(dve, waits_over)
                nc.vector.bn_stats(st[:, v % 2, :], batch(b)).then_inc(bn, 1)

            def aggregate(b, v, bn, agg, st, mv, used):
                need(dve, bn, b + 1)
                need(dve, used, b - 3)
                stand(dve, waits_over)
                nc.vector.bn_aggr(mv[:, v, :], st[:, v % 2, :]).then_inc(agg, 1)

            def step(n, u):
                s_1, s1, s2, s3, s4 = ((u + k) % 4 for k in (-1, 1, 2, 3, 4))
                p, p1, p2 = u % 2, (u + 1) % 2, u % 2
                nm = nmax[:, p1, :].rearrange("p (a j) -> p a j", a=2)
                parts = mneg[:, p1, :].rearrange("p (a q j) -> p a q j", a=2, j=HALF)
                if live(n + 3):
                    need(dve, pool_rs1, n + 4)
                    need(dve, pe_a, n + 2)
                    nc.vector.tensor_scalar(xn[:, p1, :], batch(n + 3), mv1[:, s3, 0:1], rs1[:, s3:s3 + 1],
                                            ALU.subtract, ALU.mult).then_inc(dve_xn, 1)
                if live(n + 4):
                    stats(n + 4, s4, dve_bn1, st1)
                if isinstance(n, int):
                    between(n, 0)
                if live(n - 2):
                    need(dve, pe_k, n - 1)
                    nc.vector.tensor_tensor(logits[:, bass.ds(n - 2, 1), :].rearrange("p b e -> p (b e)"),
                                            bank[BK_TAIL][:, 0:E], gbias[:], ALU.add).then_inc(dve_logit, 1)
                if live(n + 1):
                    for half, scored in enumerate((pe_d0, pe_d1)):
                        need(dve, scored, n + 2)
                        last = nc.vector.tensor_reduce(nmax[:, p1, HALF * half:HALF * half + HALF],
                                                       bank[BK_MAX + half][:].rearrange("p (h s) -> p h s", h=HALF),
                                                       AX_X, ALU.max, negate=True)
                    last.then_inc(dve_max, 1)
                if live(n + 4):
                    aggregate(n + 4, s4, dve_bn1, dve_agg1, st1, mv1, pool_rs1)
                if live(n + 1):
                    need(dve, dve_max, n + 2)
                    need(dve, pe_e, n)
                    nc.vector.tensor_copy(parts[:, :, 0, :], nm).then_inc(dve_mh, 1)
                if live(n - 1):
                    need(dve, pe_i, n)
                    nc.vector.tensor_tensor(batch(n - 1), bank[BK_TAIL][:, 0:D], batch(n - 1), ALU.add).then_inc(
                        dve_x1, 1)
                if live(n + 1):
                    need(dve, dve_mh, n + 2)
                    nc.vector.tensor_tensor(parts[:, :, 1, :], nm, parts[:, :, 0, :], ALU.subtract).then_inc(dve_mneg, 1)
                if live(n - 1):
                    need(dve, dve_x1, n)
                    stats(n - 1, s_1, dve_bn2, st2)
                if live(n - 1):
                    aggregate(n - 1, s_1, dve_bn2, dve_agg2, st2, mv2, pool_rs2)
                if live(n + 1):
                    need(dve, pe_e, n + 2)
                    need(dve, pe_f1, n)
                    nc.vector.tensor_copy(mT[:, p1, :], bank[BK_TAIL][:].bitcast(BF16)[:, 0:T]).then_inc(dve_mT, 1)
                if live(n + 2):
                    need(dve, pe_b, n + 3)
                    need(dve, pe_f1, n + 1)
                    need(dve, act_kq, n + 1)
                    for half in range(2):
                        s = slice(64 * half, 64 * half + 64)
                        last = nc.vector.scalar_tensor_tensor(
                            kz[s, p2, half, :], bank[BK_KQ][s, 0:T], colsb[s, 0:1],
                            maskr[s, bass.ds((n + 2) * T, T)], ALU.add, ALU.mult)
                    last.then_inc(dve_k, 1)
                    need(dve, pool_hm, n + 3)
                    q = bank[BK_KQ][:, T:2 * T].rearrange("p (o t) -> p o t", o=1).to_broadcast([P, HALF, T])
                    nc.vector.scalar_tensor_tensor(q4[:, p2], q, colsb[:, 1:2], headmask[:, p2], ALU.add,
                                                   ALU.mult).then_inc(dve_q, 1)
                if live(n - 1):
                    need(dve, pool_rs2, n)
                    need(dve, pe_j, n - 2)
                    need(dve, act_rows, n - 2)
                    nc.vector.tensor_scalar(x2n[:, p1, :], batch(n - 1), mv2[:, s_1, 0:1], rs2[:, s_1:s_1 + 1],
                                            ALU.subtract, ALU.mult).then_inc(dve_x2n, 1)
                if live(n + 2):
                    need(dve, dve_q, n + 3)
                    need(dve, pe_d1, n + 1)
                    nc.vector.tensor_copy(q4b[0:64, 0, p2], q4[0:64, p2]).then_inc(dve_qb, 1)
                if isinstance(n, int):
                    between(n, 1)
                pv = bank[BK_PV][:, 0:HEADS * (HD + 1)].rearrange("p (h d) -> p h d", h=HEADS)
                if live(n):
                    need(dve, pe_g, n + 1)
                    nc.vector.reciprocal(rsum[:, p, :], pv[:, :, HD]).then_inc(dve_rs, 1)
                    need(dve, dve_rs, n + 1)
                    need(dve, pe_h, n - 1)
                    nc.vector.tensor_tensor(upd[:, p, :].rearrange("p (h d) -> p h d", h=HEADS), pv[:, :, 0:HD],
                                            rsum[:, p, :].rearrange("p (h o) -> p h o", o=1).to_broadcast(
                                                [P, HEADS, HD]), ALU.mult).then_inc(dve_upd, 1)

            steps = [0]

            def link(instruction, wait=True):
                steps[0] += 1
                instruction.then_inc(route, 1)
                if wait:
                    dve.wait_ge(route, steps[0])

            def wide(ap, shape, where):
                return ap.rearrange(where, o=1).to_broadcast(shape)

            def of_group(g):
                lo, size = GROUPS[g]
                return slice(lo, lo + size), size

            def one_by_expert(shape):
                return con[:, C_REV:C_REV + E].rearrange("p (o e) -> p o e", o=1).to_broadcast(shape)

            def find(g, k):
                members, size = of_group(g)
                shape = [P, size, E]
                if k == 0:
                    dve.wait_ge(dve_logit, members.stop)
                src = lower[:, 0:size] if k else logits[:, members, :]
                eq, best = eqs[:, 0:size], top[:, k, 0:size]
                link(nc.vector.tensor_reduce(best, src, AX_X, ALU.max))
                link(nc.vector.tensor_tensor(eq, src, wide(best, shape, "p (b o) -> p b o"), ALU.is_equal))
                link(nc.vector.tensor_tensor(eq, eq, one_by_expert(shape), ALU.mult))

            def mark(g, k):
                members, size = of_group(g)
                shape = [P, size, E]
                which = first[:, k, 0:size]
                link(nc.vector.tensor_reduce(which, eqs[:, 0:size], AX_X, ALU.max))
                link(nc.vector.tensor_tensor(hot[:, k, 0:size], wide(which, shape, "p (b o) -> p b o"),
                                             one_by_expert(shape), ALU.is_equal))
                if k == 0:
                    link(nc.vector.scalar_tensor_tensor(lower[:, 0:size], hot[:, 0, 0:size], -3.0e38,
                                                        logits[:, members, :], ALU.mult, ALU.add))

            def tally(g):
                size = of_group(g)[1]
                nc.vector.tensor_tensor(gap[:, 0:size], top[:, 1, 0:size], top[:, 0, 0:size], ALU.subtract).then_inc(
                    gap_ready, 1)
                pk = picked[:, 0:E * size]
                link(nc.vector.tensor_tensor(pk.rearrange("p (e b) -> p b e", e=E), hot[:, 0, 0:size],
                                             hot[:, 1, 0:size], ALU.add))
                link(nc.vector.tensor_reduce(rowsum[:], pk.rearrange("p (e b) -> p e b", e=E), AX_X, ALU.add))
                nc.vector.tensor_copy(rowsum_b[:], rowsum[:]).then_inc(counts_in, 1)

            def number(g):
                size = of_group(g)[1]
                pk, run = picked[:, 0:E * size], running[:, 0:E * size]
                link(nc.vector.tensor_tensor_scan(run, onesf[:, 0:E * size], pk, 0.0, ALU.mult, ALU.add), wait=False)
                link(nc.vector.tensor_tensor_scan(rowinc[:], onesf[:, 0:E], rowsum[:], 0.0, ALU.mult, ALU.add))
                link(nc.vector.tensor_tensor(run, run, pk, ALU.subtract), wait=False)
                link(nc.vector.tensor_tensor(rowinc[:], rowinc[:], rowsum[:], ALU.subtract))

            def weights(g):
                members, size = of_group(g)
                dve.wait_ge(gexp_ready, g + 1)
                link(nc.vector.tensor_scalar(gden[:, 0:size], gexp[:, 0:size], 1.0, None, ALU.add))
                weight = rows[:, members, :, D + 1]
                link(nc.vector.reciprocal(weight[:, :, 0], gden[:, 0:size]))
                link(nc.vector.tensor_tensor(weight[:, :, 1], gexp[:, 0:size], weight[:, :, 0], ALU.mult))

            def whole_tiles(g, src):
                dve.wait_ge(counted, g + 1)
                nc.vector.tensor_copy(counts[:], src[:, 0:2 * E]).then_inc(counts_read, 1)
                dve.wait_ge(counts_read, g + 1)
                link(nc.vector.tensor_scalar(cnt_i[:], counts[:, E:2 * E], float(P - 1), None, ALU.add))
                link(nc.vector.tensor_scalar(cnt_i[:], cnt_i[:], P.bit_length() - 1, None, ALU.logical_shift_right))
                link(nc.vector.tensor_copy(tiles_f[:], cnt_i[:]))
                link(nc.vector.tensor_tensor_scan(tiles_inc[:], onesf[:, 0:E], tiles_f[:], 0.0, ALU.mult, ALU.add))

            def places(g):
                size = of_group(g)[1]
                link(nc.vector.tensor_tensor(place[:], tiles_inc[:], tiles_f[:], ALU.subtract))
                link(nc.vector.scalar_tensor_tensor(place[:], place[:], float(P), counts[:, 0:E], ALU.mult, ALU.add))
                link(nc.vector.tensor_tensor(place[:], place[:], rowinc[:], ALU.subtract))
                by_expert = (t[:, 0:E * size].rearrange("p (e b) -> p e b", e=E) for t in (posn, running))
                link(nc.vector.tensor_tensor(*by_expert, wide(place[:], [P, E, size], "p (e o) -> p e o"), ALU.add))

            def pick_rows(g):
                size = of_group(g)[1]
                pos = posn[:, 0:E * size].rearrange("p (o e b) -> p o b e", e=E, o=1)
                link(nc.vector.tensor_tensor(prod[:, :, 0:size], hot[:, :, 0:size],
                                             pos.to_broadcast([P, TOPK, size, E]), ALU.mult))
                link(nc.vector.tensor_reduce(dest_f[:, :, 0:size], prod[:, :, 0:size], AX_X, ALU.add))

            def end_rows(g):
                members, size = of_group(g)
                nc.vector.tensor_scalar(dest_i[:, :, members], dest_f[:, :, 0:size], float(sum(GTILES[:g]) * P), None,
                                        ALU.add).then_inc(routed, 1)

            def table(g):
                tiles, first_tile = GTILES[g], sum(GTILES[:g])
                shape = [P, tiles, E]
                link(nc.vector.tensor_tensor(
                    tcmp[:, 0:tiles], tiles_inc[:].rearrange("p (o e) -> p o e", o=1).to_broadcast(shape),
                    wide(con[:, C_TILE:C_TILE + tiles], shape, "p (i o) -> p i o"), ALU.is_le))
                link(nc.vector.tensor_reduce(texp[:, 0:tiles], tcmp[:, 0:tiles], AX_X, ALU.add))
                link(nc.vector.tensor_scalar(tile_column[:, first_tile:first_tile + tiles], texp[:, 0:tiles],
                                             float(E - 1), float(X_COLS), ALU.min, ALU.mult))

            def between(n, late):
                at = (n - ROUTE, late)
                if at == (0, 1):
                    find(0, 0)
                if at == (1, 0):
                    mark(0, 0)
                if at == (1, 1):
                    find(0, 1)
                if at == (2, 0):
                    mark(0, 1)
                if at == (2, 1):
                    tally(0)
                if at == (3, 0):
                    number(0)
                if at == (3, 1):
                    weights(0)
                if at == (4, 0):
                    whole_tiles(0, bank[BK_KQ])
                if at == (4, 1):
                    places(0)
                if at == (5, 0):
                    pick_rows(0)
                    end_rows(0)
                if at == (5, 1):
                    table(0)

            def tile_w(i, p, e):
                need(dve, pe_Y, i - 3)
                need(dve, dve_hid, i - 3)
                nc.vector.tensor_copy(wbuf[:, p, :], ew[:, bass.ds(e, X_COLS)]).then_inc(dve_w, 1)

            def after(n):
                if n in (-4, -3):
                    half = n + 4
                    row = 64 - 64 * half
                    dve.wait_ge(filled, 2)
                    nc.vector.memset(q4b[row:row + 1, half], 1.0).then_inc(filled_half, 1)
                if n == -3:
                    prepare()
                    dve.wait_ge(ld_x[1], 16)
                    dve.wait_ge(filled, 8)
                    dve.wait_ge(ld_mask[0], 16)
                if n == -2:
                    nc.vector.tensor_copy(sel_b[:], con[:, C_SEL:C_SEL + HEADS].rearrange(
                        "p (j o) -> p j o", o=1).to_broadcast([P, HEADS, P])).then_inc(idents_ready, 1)
                if n == 1:
                    dve.wait_ge(ld_small, 32)
                    dve.wait_ge(ld_mask[1], 16)
                if n == U - 1:
                    nc.vector.tensor_copy(tri_b[:], con[:, C_TRI:C_TRI + P])
                    nc.vector.tensor_copy(rows[:, :, :, D:D + 1].rearrange("p b k o -> p (b k o)").bitcast(I32), idsb[:])
                    dve.wait_ge(ld_x[2], 16)
                    dve.wait_ge(ld_x[3], 16)
                    dve.wait_ge(ld_mask[2], 16)
                    dve.wait_ge(filled_later, 4)
                if n == B:
                    dve.wait_ge(ld_ew, 32)
                    dve.wait_ge(bias_rows_e, 48)
                    for i in range(2):
                        tile_w(i, i, expert(dve, i))

            dve.wait_ge(ld_x[0], 16)
            run_attention(dve, step, after)
            for k in range(TOPK):
                find(1, k)
                mark(1, k)
            tally(1)
            number(1)
            weights(1)
            whole_tiles(1, bank[BK_PV])
            places(1)
            pick_rows(1)
            end_rows(1)
            table(1)

            def tile_hid(i, p, w):
                need(dve, act_silu, i + 1)
                need(dve, pe_H0, i + 1)
                need(dve, pe_Y, i - 1)
                for c in range(2):
                    last = nc.vector.scalar_tensor_tensor(
                        hidT[:, p, c, :], bank[BK_SC + p][:, c * P:c * P + P], wbuf[:, w, XB0 + c:XB0 + c + 1],
                        silu[:, p, c, :], ALU.add, ALU.mult)
                last.then_inc(dve_hid, 1)

            def tile_step(i, r):
                more = not isinstance(i, int) or i + 2 < TILES
                e = expert(dve, i + 2) if more else None
                tile_hid(i, r % 2, r % 4)
                if more:
                    tile_w(i + 2, (r + 2) % 4, e)

            def combine(m, k):
                lo, hi = PAIRS[m]
                if k == 0:
                    dve.wait_ge(ld_yb[m % SUMS], 16 * (m // SUMS + 1))
                if k == 1:
                    dve.wait_ge(dve_y0, m + 1)
                nc.vector.tensor_tensor(xres[:, lo:hi, :], xres[:, lo:hi, :],
                                        yb[:, m % SUMS, 0:hi - lo, k * D:k * D + D], ALU.add).then_inc(
                                            (dve_y0, dve_out)[k], 1)

            for i in range(R):
                tile_step(i, i)
            with dve.Fori(1, COMBINE) as q:
                for r in range(R):
                    tile_step(q * R + r, r)
            for i in range(COMBINE * R, TILES):
                tile_step(i, i % R)
                m = (i - COMBINE * R) // 2 - 1
                if 0 <= m < len(PAIRS):
                    combine(m, i % 2)
            for i, (lo, hi) in enumerate(LAST):
                dve.wait_ge(ld_last[i], 16)
                for k in range(TOPK):
                    if k:
                        dve.wait_ge(dve_y0, len(PAIRS) + i + 1)
                    nc.vector.tensor_tensor(xres[:, lo:hi, :], xres[:, lo:hi, :],
                                            landing(lo, hi)[:, :, k * D:k * D + D], ALU.add).then_inc((dve_y0, dve_last)[k], 1)

        @block.tensor
        def _(pe):
            ident = con[:, C_IDENT:C_IDENT + P]
            def mm(o, lhsT, rhs, start=True, stop=True):
                return nc.tensor.matmul(o, lhsT, rhs, start=start, stop=stop)

            def step(n, u):
                if live(n):
                    scores(n, u, 0)
                if live(n - 1):
                    weighted(n - 1, (u - 1) % 2, 1)
                if live(n + 2):
                    need(pe, dve_xn, n + 3)
                    need(pe, act_xnT, n + 2)
                    nc.tensor.transpose(bank[BK_XT][:, 0:T], xn[:, u % 2, :], ident).then_inc(pe_a, 1)
                if live(n - 2):
                    need(pe, dve_x2n, n - 1)
                    need(pe, dve_mT, upto(n + 1))
                    nc.tensor.transpose(bank[BK_TAIL][:, 0:T], x2n[:, u % 2, :], ident).then_inc(pe_j, 1)
                if live(n):
                    scores(n, u, 1)
                else:
                    gate_logits(n, u)
                if live(n + 1):
                    p = (u + 1) % 2
                    need(pe, act_kq, n + 2)
                    need(pe, dve_qb, n + 2)
                    need(pe, dve_max, n + 1)
                    for half, done in enumerate((pe_d0, pe_d1)):
                        dst = bank[BK_MAX + half]
                        keys = kb[:, half, bass.ds(n + 1, 1), :].rearrange("p b s -> p (b s)")
                        for j in range(HALF):
                            last = mm(dst[:, j * T:j * T + T], q4b[:, half, p, j, :], keys)
                        last.then_inc(done, 1)
                if live(n - 1):
                    need(pe, dve_upd, n)
                    need(pe, dve_logit, n - 1)
                    nc.tensor.transpose(bank[BK_TAIL][:, 0:T], upd[:, (u - 1) % 2, :], ident).then_inc(pe_h, 1)
                if live(n + 1):
                    r = (u + 1) % 4
                    need(pe, dve_upd, n)
                    if isinstance(n, int) and n == 0:
                        pe.wait_ge(act_v, 1)
                    need(pe, ld_ctx[r], ctx_loads(n, u, 1))
                    dst = bank[BK_PV][:, 0:D]
                    for c in range(2):
                        mm(dst, ctx[:, r, c, :], wat[:, WV + D * c:WV + D * c + D], start=c == 0, stop=False)
                    mm(dst, ones_b[:], bias3[:, BV:BV + D], start=False).then_inc(pe_c, 1)
                if live(n - 1):
                    dst = bank[BK_TAIL][:, 0:D]
                    need(pe, act_updT, n)
                    mm(dst, updT[:, (u - 1) % 2, :], wat[:, WO + D:WO + 2 * D], stop=False)
                    mm(dst, xnT[:, (u - 1) % 4, :], wat[:, WO:WO + D], start=False, stop=False)
                    mm(dst, ones_b[:], bias3[:, BO:BO + D], start=False).then_inc(pe_i, 1)
                if live(n + 2):
                    r = (u + 2) % 4
                    need(pe, ld_ctx[r], ctx_loads(n, u, 2))
                    need(pe, act_xnT, n + 3)
                    need(pe, dve_q, n + 2)
                    if isinstance(n, int) and n == ROUTE + 4:
                        pe.wait_ge(counts_read, 1)
                    for c in range(2):
                        mm(bank[BK_KQ][:, 0:T], wat[:, WK + D * c:WK + D * c + D], ctx[:, r, c, :], start=c == 0,
                           stop=c == 1)
                    mm(bank[BK_KQ][:, T:2 * T], wat[:, WQ:WQ + D], xnT[:, r, :]).then_inc(pe_b, 1)
                if live(n + 1):
                    need(pe, dve_mneg, n + 2)
                    need(pe, dve_x1, n)
                    nc.tensor.transpose(bank[BK_TAIL][:].bitcast(BF16)[:, 0:T], mneg[:, (u + 1) % 2, :],
                                        ident_b[:]).then_inc(pe_e, 1)
                if live(n):
                    need(pe, act_v, upto(n + 2))
                    weighted(n, u % 2, 0)

            def ctx_loads(n, u, ahead):
                if isinstance(n, int):
                    return 16 * ((n + ahead) // 4 + 1)
                return (n - u) * 4 + 16 * ((u + ahead) // 4 + 1)

            def weighted(n, p, half):
                need(pe, (act_exp0, act_exp1)[half], n + 1)
                for h in range(HALF * half, HALF * half + HALF):
                    last = mm(bank[BK_PV][:, h * (HD + 1):(h + 1) * (HD + 1)], attn[:, p, h, :], vaug[:, p, h, :])
                if half == 1:
                    last.then_inc(pe_g, 1)

            def gate_logits(n, u):
                if isinstance(n, int) and n == ROUTE + 4:
                    pe.wait_ge(dve_q, n + 2)
                    count(0, bank[BK_KQ])
                if live(n - 2):
                    need(pe, act_x2T, n - 1)
                    mm(bank[BK_TAIL][:, 0:E], x2T[:, u % 2, :], wat[:, WG:WG + E]).then_inc(pe_k, 1)

            def scores(n, u, half):
                p = u % 2
                dst = bank[BK_SC + half]
                if half == 0:
                    need(pe, dve_mT, n + 1)
                need(pe, (act_exp0, act_exp1)[half], n)
                mm(dst[:].rearrange("p (h t) -> p h t", h=HALF), kz[:, p, half, :], q4[:, p], stop=False)
                if half == 1:
                    gate_logits(n, u)
                for j in range(HALF):
                    last = mm(dst[:, j * T:j * T + T], sel_b[:, HALF * half + j, :], mT[:, p, :], start=False, stop=j == HALF - 1)
                last.then_inc((pe_f0, pe_f1)[half], 1)

            def count(g, dst):
                pe.wait_ge(counts_in, g + 1)
                mm(dst[:, 0:E], tri_b[:], rowsum_b[:])
                mm(dst[:, E:2 * E], ones_b[:], rowsum_b[:]).then_inc(counted, 1)

            def after(n):
                if n == -3:
                    pe.wait_ge(ld_con, 16)
                    pe.wait_ge(ld_w, 16)
                if n == -2:
                    pe.wait_ge(filled, 8)
                    pe.wait_ge(filled_half, 3)
                    pe.wait_ge(mask_rows, 32)
                    pe.wait_ge(bias_rows, 48)
                    pe.wait_ge(idents_ready, 1)
                if n == -1:
                    pe.wait_ge(idents_ready, 2)

            run_attention(pe, step, after)

            def tile_T(i, r, q):
                need(pe, ld_xs[r], (q + 1) * 16)
                need(pe, act_exT, i - 1)
                nc.tensor.transpose(bank[(BK_XT, BK_TAIL)[r % 2]][:, 0:P], xs[:, r, 0:D], ident).then_inc(pe_T, 1)

            def tile_H(i, p, w):
                need(pe, act_exT, i + 1)
                need(pe, dve_w, i + 1)
                need(pe, act_silu, i - 1)
                for c in range(2):
                    last = mm(bank[BK_MAX + p][:, c * P:c * P + P], wbuf[:, w, X1 + c * P:X1 + c * P + P], exT[:, p, :])
                last.then_inc(pe_H1, 1)
                need(pe, dve_hid, i - 1)
                for c in range(2):
                    last = mm(bank[BK_SC + p][:, c * P:c * P + P], wbuf[:, w, X0 + c * P:X0 + c * P + P], exT[:, p, :])
                last.then_inc(pe_H0, 1)

            def tile_Y(i, p, w):
                need(pe, dve_hid, i + 1)
                need(pe, act_y, i - 1)
                dst = bank[(BK_KQ, BK_PV)[p]][:, 0:D]
                for c in range(2):
                    mm(dst, hidT[:, p, c, :], wbuf[:, w, X2 + c * D:X2 + c * D + D], start=c == 0, stop=False)
                mm(dst, ones_b[:], wbuf[:, w, XB2:X1].bitcast(BF16), start=False).then_inc(pe_Y, 1)

            def tile_step(i, r, q):
                static = isinstance(i, int)
                if not static or i < TILES:
                    tile_H(i, r % 2, r % 4)
                if not static or i >= 1:
                    tile_Y(i - 1, (r - 1) % 2, (r - 1) % 4)
                if not static or i + 2 < TILES:
                    tile_T(i + 2, (r + 2) % R, q if r < R - 2 else q + 1)

            pe.wait_ge(dve_logit, B)
            pe.wait_ge(dve_upd, B)
            count(1, bank[BK_PV])
            tile_T(0, 0, 0)
            tile_T(1, 1, 0)
            for i in range(R):
                if i == 2:
                    pe.wait_ge(counts_read, 2)
                tile_step(i, i, 0)
            with pe.Fori(1, TILES // R) as q:
                for r in range(R):
                    tile_step(q * R + r, r, q)
            for i in range(TILES // R * R, TILES + 1):
                tile_step(i, i % R, i // R)


def kernel(**inputs):
    import numpy as np
    import concourse.bacc as bacc
    from concourse.bass_utils import run_bass_kernel_spmd

    def get(name):
        return np.asarray(inputs[name])

    def c(a):
        return np.ascontiguousarray(a)

    x, context, mask = get("x"), get("ctx_2048"), get("mask_BxS2_fk1")
    w_src, w_tgt, w_out = get("L0_xattn_W_src"), get("L0_xattn_W_tgt"), get("L0_xattn_W_out")
    b_src = get("L0_xattn_b_src")
    ctxT = c(context.transpose(0, 2, 1).reshape(B, 2, P, T).transpose(0, 2, 1, 3))
    wkT, wvT = w_src[:D].T.reshape(2, P, D), w_src[D:].T.reshape(2, P, D)
    woT = w_out.T.reshape(2, P, D)
    w_attn = c(np.concatenate([wkT[0], wkT[1], wvT[0], wvT[1], w_tgt.T, woT[0], woT[1], get("L0_ffn_gate_w").T], 1))
    cols = c(np.concatenate([b_src[:D, None], get("L0_xattn_b_tgt")[:, None], mask.T], 1))
    biases = c(np.concatenate([b_src[None, D:], get("L0_xattn_b_out")[None], get("L0_ffn_b2")], 0))
    wx = [np.concatenate([get("L0_ffn_w" + k).transpose(2, 0, 1),
                          get("L0_ffn_b" + k).reshape(E, H // P, P).transpose(2, 0, 1)], 2) for k in "01"]
    w2 = get("L0_ffn_w2").reshape(E, D, 2, P).transpose(3, 0, 2, 1).reshape(P, E, 2 * D)
    p = np.arange(P)
    consts = np.zeros((P, C_COLS), np.float32)
    consts[:, C_IDENT:C_IDENT + P] = np.eye(P)
    consts[:, C_TRI:C_TRI + P] = p[:, None] < p[None, :]
    consts[:, C_PATT:C_PATT + HALF] = (p % 64 // HD)[:, None] == np.arange(HALF)[None, :]
    consts[:, C_SEL:C_SEL + HEADS] = (p // 64 * HALF + p % HALF)[:, None] == np.arange(HEADS)[None, :]
    consts[:, C_REV:C_REV + E] = E - np.arange(E)[None, :]
    consts[:, C_TILE:C_TILE + GT] = np.arange(GT)[None, :]
    token = (np.arange(B)[None, :, None] * T + p[:, None, None]) * TOPK + np.arange(TOPK)[None, None, :]
    arrays = {
        "x": c(x), "ctxT": ctxT, "w_attn": w_attn, "cols": cols, "mask": c(mask), "mask_row": c(mask.reshape(1, -1)[0]),
        "gate_b": c(get("L0_ffn_gate_b")), "biases": biases, "w02": c(np.concatenate([wx[0], w2], 2)), "w1": c(wx[1]), "consts": consts,
        "ids": c(token.reshape(P, B * TOPK).astype(np.int32)),
    }
    nc = bacc.Bacc("TRN2", target_bir_lowering=False, num_devices=1)
    handles = {k: nc.dram_tensor(k, v.shape, mybir.dt.from_np(v.dtype), kind="ExternalInput").ap()
               for k, v in arrays.items()}
    out = nc.dram_tensor("out", (B, T, D), F32, kind="ExternalOutput").ap()
    build(nc, *handles.values(), out)
    r = run_bass_kernel_spmd(nc, [arrays], core_ids=[0])
    return r.results[0]["out"]
```
